# Optimizing a Trainium2 kernel written in Bass

```python
import numpy as np
import jax
import jax.numpy as jnp

def _softmax(x, axis=-1):
    return jax.nn.softmax(x, axis=axis)

def _gelu(x):
    return jax.nn.gelu(x, approximate=True)

def _silu(x):
    return jax.nn.silu(x)

def _sigmoid(x):
    return jax.nn.sigmoid(x)

def _layernorm(x, axis=-1, eps=1e-05):
    m = jnp.mean(x, axis=axis, keepdims=True)
    v = jnp.var(x, axis=axis, keepdims=True)
    return (x - m) / jnp.sqrt(v + eps)

def _scatter_add(tgt, idx, src, axis=0):
    return tgt.at[idx].add(src)

def _segment_sum(src, seg, n):
    return jax.ops.segment_sum(src, seg, n)
kernel_name = 'mk_gnn_preln_d1_gnn_r64_7d6331'

def setup_inputs(seed: int=0):
    np.random.seed(seed)
    _w = jnp.asarray

    def _rec_inputs():
        import jax
        import jax.numpy as jnp
        _gk = jax.random.key(seed)
        x = -0.000202 + 1 * jax.random.normal(jax.random.fold_in(_gk, 1), (100000, 128), jnp.float32)
        src = jax.random.randint(jax.random.fold_in(_gk, 2), (25000,), 0, 100000, jnp.int32)
        dst = jnp.minimum((100000 * jax.random.uniform(jax.random.fold_in(_gk, 3), (25000,)) ** 2.0).astype(jnp.int32), 99999)
        _o = jnp.argsort(dst, stable=True)
        src = src[_o]
        dst = dst[_o]
        edge_attr_20 = -8.62073e-06 + 0.999901 * jax.random.normal(jax.random.fold_in(_gk, 12), (25000, 20), jnp.float32)
        edge_weight = jax.random.uniform(jax.random.fold_in(_gk, 13), (25000,), jnp.float32, 0.0, 0.999999)
        return (x, src, dst, edge_attr_20, edge_weight)
    x, src, dst, edge_attr_20, edge_weight = _rec_inputs()

    def _L0_gnn_setup():
        import jax, jax.numpy as jnp
        import numpy as np
        N_ATOMS = 50000
        N_EDGES = 25000
        N_BASIS = 128
        N_RBF = 20
        N_FILT = 128
        LOG2 = float(np.log(2.0))

        def ssp(t):
            return jax.nn.softplus(t) - LOG2
        key = jax.random.key(seed)
        ks = jax.random.split(key, 12)
        s = lambda fan_in: 1.0 / np.sqrt(fan_in)
        return {'x': jax.random.normal(ks[0], (N_ATOMS, N_BASIS), dtype=jnp.float32), 'f_ij': jax.random.normal(ks[1], (N_EDGES, N_RBF), dtype=jnp.float32), 'rcut_ij': jax.random.uniform(ks[2], (N_EDGES,), dtype=jnp.float32), 'idx_i': jnp.sort(jax.random.randint(ks[3], (N_EDGES,), 0, N_ATOMS)), 'idx_j': jax.random.randint(ks[4], (N_EDGES,), 0, N_ATOMS), 'W_in2f': jax.random.normal(ks[5], (N_BASIS, N_FILT), dtype=jnp.float32) * s(N_BASIS), 'W_f1': jax.random.normal(ks[6], (N_RBF, N_FILT), dtype=jnp.float32) * s(N_RBF), 'b_f1': jnp.zeros((N_FILT,), dtype=jnp.float32), 'W_f2': jax.random.normal(ks[7], (N_FILT, N_FILT), dtype=jnp.float32) * s(N_FILT), 'b_f2': jnp.zeros((N_FILT,), dtype=jnp.float32), 'W_o1': jax.random.normal(ks[8], (N_FILT, N_BASIS), dtype=jnp.float32) * s(N_FILT), 'b_o1': jnp.zeros((N_BASIS,), dtype=jnp.float32), 'W_o2': jax.random.normal(ks[9], (N_BASIS, N_BASIS), dtype=jnp.float32) * s(N_BASIS), 'b_o2': jnp.zeros((N_BASIS,), dtype=jnp.float32)}
    _L0_gnn_all = _L0_gnn_setup()
    _L0_gnn_in = {k: v for k, v in _L0_gnn_all.items() if k in ('W_in2f', 'W_f1', 'b_f1', 'W_f2', 'b_f2', 'W_o1', 'b_o1', 'W_o2', 'b_o2')}
    del _L0_gnn_all
    return {'x': x, 'src': src, 'dst': dst, 'edge_attr_20': edge_attr_20, 'edge_weight': edge_weight, 'L0_gnn_W_in2f': _L0_gnn_in['W_in2f'], 'L0_gnn_W_f1': _L0_gnn_in['W_f1'], 'L0_gnn_b_f1': _L0_gnn_in['b_f1'], 'L0_gnn_W_f2': _L0_gnn_in['W_f2'], 'L0_gnn_b_f2': _L0_gnn_in['b_f2'], 'L0_gnn_W_o1': _L0_gnn_in['W_o1'], 'L0_gnn_b_o1': _L0_gnn_in['b_o1'], 'L0_gnn_W_o2': _L0_gnn_in['W_o2'], 'L0_gnn_b_o2': _L0_gnn_in['b_o2']}

def reference(x, src, dst, edge_attr_20, edge_weight, L0_gnn_W_in2f, L0_gnn_W_f1, L0_gnn_b_f1, L0_gnn_W_f2, L0_gnn_b_f2, L0_gnn_W_o1, L0_gnn_b_o1, L0_gnn_W_o2, L0_gnn_b_o2):
    import jax
    import jax.numpy as jnp

    def _L0_gnn_ref(x, f_ij, rcut_ij, idx_i, idx_j, W_in2f, W_f1, b_f1, W_f2, b_f2, W_o1, b_o1, W_o2, b_o2):
        import jax, jax.numpy as jnp
        import numpy as np
        N_ATOMS = 50000
        N_EDGES = 25000
        N_BASIS = 128
        N_RBF = 20
        N_FILT = 128
        LOG2 = float(np.log(2.0))

        def ssp(t):
            return jax.nn.softplus(t) - LOG2
        n_atoms = x.shape[0]
        h = x @ W_in2f
        Wij = ssp(f_ij @ W_f1 + b_f1) @ W_f2 + b_f2
        Wij = Wij * rcut_ij[:, None]
        x_ij = h[idx_j] * Wij
        agg = jax.ops.segment_sum(x_ij, idx_i, num_segments=n_atoms)
        out = ssp(agg @ W_o1 + b_o1) @ W_o2 + b_o2
        return out
    h = jnp.maximum(_layernorm(x, axis=-1), 0.0)
    x = x + _L0_gnn_ref(h, edge_attr_20, edge_weight, src, dst, L0_gnn_W_in2f, L0_gnn_W_f1, L0_gnn_b_f1, L0_gnn_W_f2, L0_gnn_b_f2, L0_gnn_W_o1, L0_gnn_b_o1, L0_gnn_W_o2, L0_gnn_b_o2)
    return x

_drawn_inputs = setup_inputs


def setup_inputs(seed=0):
    import zlib

    import numpy as np

    out = dict(_drawn_inputs(seed))
    spreads = {'L0_gnn_b_f1': (0.0, 0.8),
     'L0_gnn_b_f2': (0.0, 0.634),
     'L0_gnn_b_o1': (0.0, 0.1),
     'L0_gnn_b_o2': (0.0, 0.1)}
    factors = {}
    for name, (base, spread) in spreads.items():
        noise = np.random.default_rng([zlib.crc32(name.encode()), seed]).standard_normal(out[name].shape)
        drawn = base * np.exp(spread * noise) if base else spread * noise
        out[name] = jnp.asarray(drawn.astype(out[name].dtype))
    for name, factor in factors.items():
        out[name] = (out[name] * factor).astype(out[name].dtype)
    return out
```

```python
import math
from contextlib import ExitStack

import concourse.bass as bass
from concourse import mybir

F32 = mybir.dt.float32
BF16 = mybir.dt.bfloat16
I32 = mybir.dt.int32
ALU = mybir.AluOpType
ACT = mybir.ActivationFunctionType

P = 128
NODES = 100000
EDGES = 25000
D = 128
RBF = 20
LN_EPS = 1e-5
LN2 = math.log(2.0)
EXP_CAP = 2.0**60
RSQRT_MAGIC = float(0x5F3759DF)
NEWTON = 3

TPC = 4
CHUNK = TPC * P
CHUNKS = -(-EDGES // CHUNK)
TILES = CHUNKS * TPC
GROUP = 7
GROUPS = CHUNKS // GROUP
GT = GROUP * TPC
TAIL = EDGES - (CHUNKS - 1) * CHUNK

ZROWS = 2048
ZBLOCKS = -(-NODES // ZROWS)
DUMP = ZBLOCKS * ZROWS

CLEAR_GROUPS = 1 + (ZBLOCKS - GROUP) // (2 * GROUP)
assert GROUP + 2 * GROUP * (CLEAR_GROUPS - 1) == ZBLOCKS

ROWS = 1024
RPP = ROWS // P
BLOCK = RPP * D
BLOCKS = -(-NODES // ROWS)
HALVES = 2 * BLOCKS
SLOTS = 7
LAG = 2
BGROUP = SLOTS
BGROUPS = BLOCKS // BGROUP
HGROUP = 2 * BGROUP

assert CHUNKS == GROUP * GROUPS and BLOCKS == BGROUP * BGROUPS and ROWS == 2 * TPC * P


def gnn_layer(nc, x, src, dst, edge_attr, edge_weight, w_in2f, w_f1, b_f1, w_f2, b_f2, w_o1, b_o1, w_o2, b_o2, out):
    agg = nc.dram_tensor("agg", (DUMP + CHUNK, D), F32, kind="Internal").ap()
    src_padded = nc.dram_tensor("src_padded", (CHUNKS, CHUNK), I32, kind="Internal").ap()

    with ExitStack() as ctx:

        def sb(name, shape, dt=F32):
            return ctx.enter_context(nc.sbuf_tensor(name, shape, dt))

        def ps(name):
            return ctx.enter_context(nc.psum_tensor(name, [P, CHUNK], F32))

        def sem(name):
            return ctx.enter_context(nc.semaphore(name))

        rows_io = sb("rows_io", [P, TILES * D])
        agg_in_sb = rows_io[:, 0 : SLOTS * BLOCK].rearrange("p (k f) -> p k f", k=SLOTS)
        x_sb = sb("x_sb", [P, SLOTS, BLOCK])
        feats = sb("feats", [P, CHUNKS, TPC * RBF])
        src_all = sb("src_all", [P, GROUP, CHUNK], I32)
        dst_idx = sb("dst_idx", [P, TILES], I32)
        agg_idx = sb("agg_idx", [P, TILES], I32)
        src_cols = sb("src_cols", [P, 2, TILES])
        weight = sb("weight", [P, TILES])
        dump_row = sb("dump_row", [P, TPC])
        stats = sb("stats", [P, GT, 6])
        mean = sb("mean", [P, GT])
        per_edge = sb("per_edge", [P, 3, TPC + GT])
        scale, src_now, src_less_dump = (per_edge[:, i, :] for i in range(3))
        later = sb("later", [P, TPC])
        picked = sb("picked", [P, TPC])
        var = sb("var", [P, GT])
        ln_a = sb("ln_a", [P, GT])
        ln_b = sb("ln_b", [P, GT])
        rsq = sb("rsq", [P, GT])
        h = sb("h", [P, CHUNK])
        hT = sb("hT", [P, CHUNK])
        g = sb("g", [P, CHUNK])
        feat_in = sb("feat_in", [P, TPC * RBF])
        featT = sb("featT", [TPC * RBF, P])
        soft1 = sb("soft1", [P, CHUNK])
        act1 = sb("act1", [P, CHUNK])
        msg = sb("msg", [P, CHUNK])
        pairs = [sb(f"pairs{j}", [P, CHUNK - j * P]) for j in range(TPC)]
        aggT = [sb(f"aggT{k}", [P, CHUNK]) for k in range(2)]
        soft2 = [sb(f"soft2{k}", [P, CHUNK]) for k in range(2)]
        act2 = [sb(f"act2{k}", [P, CHUNK]) for k in range(2)]
        ident = sb("ident", [P, P])
        ones_bf = sb("ones_bf", [P, P], BF16)
        w_in = sb("w_in", [P, D])
        w1_at = sb("w1_at", [TPC * RBF, TPC, D])
        w2 = sb("w2", [P, D])
        wo1 = sb("wo1", [P, D])
        wo2 = sb("wo2", [P, D])
        half = sb("half", [P, 1])
        b1 = sb("b1", [P, 1])
        bo1 = sb("bo1", [P, 1])
        b1_ln2 = sb("b1_ln2", [P, 1])
        bo1_ln2 = sb("bo1_ln2", [P, 1])
        bias_rows = [sb(f"bias_rows{k}", [P, D]) for k in range(2)]
        bias_bf = [sb(f"bias_bf{i}", [P, D], BF16) for i in range(3)]
        bias_parts = [sb(f"bias_parts{k}", [P, D], BF16) for k in range(2)]

        dst_rows = hT[:, :].bitcast(I32)
        dst_rows_f = g
        src_rows = act1[:, :].bitcast(I32)
        src_rows_f = soft1
        weight_rows = msg
        zeros = x_sb[:, 0:2, :]
        later_mask = x_sb[:, 2, 0:CHUNK]
        dump_i = x_sb[:, 3, 0:TPC].bitcast(I32)

        bank = [ps(f"bank{k}") for k in range(7)]
        ps_mask = ps("ps_mask")
        ps_hT, ps_g, ps_a1, ps_w, ps_sum = bank[0:5]
        ps_fT = ps_hT[0 : TPC * RBF, 0:P]
        ps_aggT, ps_z2, ps_o = bank[0:2], bank[2:4], bank[4:6]

        s_mine = sem("s_mine")
        s_init = sem("s_init")
        s_dst = sem("s_dst")
        s_src = sem("s_src")
        s_pad = sem("s_pad")
        s_wts = sem("s_wts")
        s_par = sem("s_par")
        s_bias = sem("s_bias")
        s_feat = sem("s_feat")
        s_zero = sem("s_zero")
        s_ident = sem("s_ident")
        s_iota = sem("s_iota")
        s_prep = sem("s_prep")
        s_pprep = sem("s_pprep")
        agg_done = sem("agg_done")
        gathered = [sem(f"gathered{c}") for c in range(GROUP)]
        scattered = sem("scattered")
        src_in = [sem(f"src_in{c}") for c in range(GROUP)]
        x_in = [sem(f"x_in{k}") for k in range(SLOTS)]
        agg_in = [sem(f"agg_in{k}") for k in range(SLOTS)]
        stored = [sem(f"stored{k}") for k in range(SLOTS)]
        bn_done = sem("bn_done")
        ln_step = sem("ln_step")
        h_done = sem("h_done")
        hT_ps = sem("hT_ps")
        hT_sb = sem("hT_sb")
        g_ps = sem("g_ps")
        g_sb = sem("g_sb")
        feat_sb = sem("feat_sb")
        fT_ps = sem("fT_ps")
        fT_sb = sem("fT_sb")
        a1_ps = sem("a1_ps")
        exp1 = sem("exp1")
        cap1 = sem("cap1")
        log1 = sem("log1")
        act1_sb = sem("act1_sb")
        w_ps = sem("w_ps")
        pairs_sb = sem("pairs_sb")
        picked_sb = sem("picked_sb")
        msg_sb = sem("msg_sb")
        sum_ps = sem("sum_ps")
        msgs_ready = sem("msgs_ready")
        aggT_ps = sem("aggT_ps")
        aggT_sb = sem("aggT_sb")
        z2_ps = sem("z2_ps")
        exp2 = sem("exp2")
        cap2 = sem("cap2")
        log2 = sem("log2")
        act2_sb = sem("act2_sb")
        o_ps = sem("o_ps")
        added = sem("added")

        block = ctx.enter_context(nc.Block())

        def tile_cols(t):
            return bass.ds(t * D, D)

        def block_rows(ap, m):
            at = min(m * ROWS, NODES - ROWS) if isinstance(m, int) else m * ROWS
            return ap[bass.ds(at, ROWS), :].rearrange("(p r) d -> p (r d)", p=P)

        full = CHUNKS - 1
        full_edges = full * CHUNK

        @block.sync
        def _(sp):
            def load_rows(tile, v, s):
                sp.dma_start(tile[0:full, :], v[0:full_edges].rearrange("(n i) -> n i", i=CHUNK)).then_inc(s, 16)
                sp.dma_start(tile[full:CHUNKS, 0:TAIL], v[full_edges:EDGES].rearrange("(n i) -> n i", n=1)).then_inc(s, 16)

            sp.wait_ge(s_init, 1)
            load_rows(dst_rows, dst, s_dst)
            sp.wait_ge(s_init, 2)
            load_rows(src_rows, src, s_src)
            sp.wait_ge(s_init, 3)
            load_rows(weight_rows, edge_weight, s_wts)
            for tile, v in ((b1, b_f1), (bo1, b_o1)):
                sp.dma_start(tile[:, :], v.rearrange("(p a) -> p a", a=1)).then_inc(s_bias, 16)
            for tile, v in zip(bias_rows, (b_f2, b_o2)):
                sp.dma_start(tile[:, :], v.rearrange("(a d) -> a d", a=1).to_broadcast([P, D])).then_inc(s_bias, 16)
            for tile, v in ((w_in, w_in2f), (w2, w_f2), (wo1, w_o1), (wo2, w_o2)):
                sp.dma_start(tile[:, :], v[:, :]).then_inc(s_par, 16)
            sp.wait_ge(s_init, 5)
            for i in range(TPC):
                sp.dma_start(w1_at[i * RBF : (i + 1) * RBF, i, :], w_f1[:, :]).then_inc(s_par, 16)
            by_quad = edge_attr[0:full_edges, :].rearrange("(n q i) k -> q n (i k)", q=P, i=TPC)
            sp.dma_start(feats[:, 0:full, :], by_quad).then_inc(s_feat, 16)
            sp.dma_start(feats[0 : TAIL // TPC, full, :], edge_attr[full_edges:EDGES, :].rearrange("(q i) k -> q (i k)", i=TPC)).then_inc(s_feat, 16)
            sp.wait_ge(s_src, 32)
            sp.dma_start(src_padded[:, :], src_rows[0:CHUNKS, :]).then_inc(s_pad, 16)
            sp.wait_ge(s_pad, 16)

            def load_src(n, c):
                sp.dma_start(src_all[:, c, :], src_padded[bass.ds(n, 1), :].to_broadcast([P, CHUNK])).then_inc(src_in[c], 16)

            for c in range(GROUP):
                load_src(c, c)
            sp.wait_ge(s_init, 6)

            def clear(zb):
                sp.dma_start(agg[bass.ds(zb * ZROWS, ZROWS), :].rearrange("(p r) d -> p (r d)", p=P), zeros).then_inc(s_zero, 16)

            dump = agg[DUMP : DUMP + CHUNK, :].rearrange("(p r) d -> p (r d)", p=P)
            sp.dma_start(dump, x_sb[:, 0, 0:CHUNK]).then_inc(s_zero, 16)
            for zb in range(GROUP):
                clear(zb)

            def next_src(group, clears):
                for c in range(GROUP):
                    n = group * GROUP + c
                    sp.wait_ge(pairs_sb, n - GROUP + 1)
                    load_src(n, c)
                    for i in range(clears):
                        clear(n * clears - GROUP * (clears - 1) + i)

            with sp.Fori(1, CLEAR_GROUPS) as group:
                next_src(group, 2)
            with sp.Fori(CLEAR_GROUPS, GROUPS) as group:
                next_src(group, 0)

            def load_x(m, k):
                sp.dma_start(x_sb[:, k, :], block_rows(x, m)).then_inc(x_in[k], 16)

            def load_agg(m, k):
                sp.dma_start(agg_in_sb[:, k, :], block_rows(agg, m)).then_inc(agg_in[k], 16)

            sp.wait_ge(s_zero, 16 * (ZBLOCKS + 1))
            sp.wait_ge(s_prep, 5)
            for m in range(SLOTS - LAG):
                load_x(m, m)
            sp.wait_ge(agg_done, 1)
            for m in range(SLOTS - LAG):
                load_agg(m, m)

            def turn(group, first=False, last=False):
                for k in range(BGROUP):
                    m = group * BGROUP + k
                    sp.wait_ge(added, 2 * m + 2)
                    if last and k == BGROUP - 1:
                        sp.wait_ge(stored[k - 1], 16 * BGROUPS)
                    sp.dma_start(block_rows(out, m), x_sb[:, k, :]).then_inc(stored[k], 16)
                    back = k - LAG
                    if back >= 0:
                        sp.wait_ge(stored[back], group * 16 + 16)
                    elif not first:
                        sp.wait_ge(stored[back % BGROUP], group * 16)
                    if not (last and back >= 0):
                        load_x(m + SLOTS - LAG, back % BGROUP)
                        load_agg(m + SLOTS - LAG, back % BGROUP)

            turn(0, first=True)
            with sp.Fori(1, BGROUPS - 1) as group:
                turn(group)
            turn(BGROUPS - 1, last=True)
            for k in range(BGROUP - LAG, BGROUP):
                sp.wait_ge(stored[k], 16 * BGROUPS)

        @block.gpsimd
        def _(gp):
            gp.memset(ident[:, :], 0.0).then_inc(s_ident, 1)
            gp.memset(later_mask, 0.0).then_inc(s_ident, 1)
            gp.wait_ge(s_ident, 2)
            gp.affine_select(out=ident[:, :], in_=ident[:, :], compare_op=ALU.not_equal, fill=1.0, base=0, pattern=[[-1, P]], channel_multiplier=1).then_inc(s_ident, 1)
            gp.affine_select(out=later_mask, in_=later_mask, compare_op=ALU.is_ge, fill=1.0, base=0, pattern=[[-1, CHUNK]], channel_multiplier=1).then_inc(s_ident, 1)
            gp.iota(dump_i, pattern=[[P, TPC]], base=DUMP, channel_multiplier=1).then_inc(s_iota, 1)
            gp.memset(ones_bf[:, :], 1.0).then_inc(s_iota, 1)

            gp.wait_ge(s_prep, 2)
            for t in range(TILES):
                chunk = t // TPC
                c = chunk % GROUP
                if t % TPC == 0 and chunk >= GROUP:
                    gp.wait_ge(gathered[c], 16 * TPC * (chunk // GROUP))
                gp.indirect_dma_start(
                    rows_io[:, t * D : (t + 1) * D], None, x[:, :], bass.IndirectOffsetOnAxis(dst_idx[:, t : t + 1], 0)
                ).then_inc(gathered[c], 16)

            gp.wait_ge(s_zero, 16 * (ZBLOCKS + 1))
            for t in range(TILES):
                chunk, j = divmod(t, TPC)
                if j == 0:
                    gp.wait_ge(msgs_ready, chunk + 1)
                    if chunk:
                        gp.wait_ge(scattered, 16 * TPC * chunk)
                gp.indirect_dma_start(
                    agg[:, :], bass.IndirectOffsetOnAxis(agg_idx[:, t : t + 1], 0), rows_io[:, t * D : (t + 1) * D], None, compute_op=ALU.add
                ).then_inc(scattered, 16)
            gp.wait_ge(scattered, 16 * TILES)
            gp.sem_inc(agg_done, 1)

        @block.scalar
        def _(act):
            def copy_feats(n):
                act.activation(feat_in[:, :], feats[:, bass.ds(n, 1), :].rearrange("q n k -> q (n k)"), ACT.Copy).then_inc(feat_sb, 1)

            def evac_featT(n):
                act.wait_ge(fT_ps, n + 1)
                act.activation(featT[:, :], ps_fT, ACT.Copy).then_inc(fT_sb, 1)

            def exp_1(n):
                act.wait_ge(a1_ps, n + 1)
                act.activation(soft1[:, :], ps_a1[:, :], ACT.Exp, bias=b1[:, :]).then_inc(exp1, 1)

            def log_1(n):
                act.wait_ge(cap1, n + 1)
                act.activation(soft1[:, :], soft1[:, :], ACT.Ln, bias=half[:, :], scale=0.5).then_inc(log1, 1)

            def evac_hT(n):
                act.wait_ge(hT_ps, n + 1)
                act.activation(hT[:, :], ps_hT[:, :], ACT.Copy).then_inc(hT_sb, 1)

            def evac_g(n, first=False):
                if not first:
                    act.wait_ge(msg_sb, n)
                act.wait_ge(g_ps, n + 1)
                act.activation(g[:, :], ps_g[:, :], ACT.Copy).then_inc(g_sb, 1)

            def step(n, first=False, ahead=2):
                evac_hT(n)
                log_1(n)
                evac_g(n, first)
                if ahead >= 1:
                    evac_featT(n + 1)
                if ahead >= 2:
                    copy_feats(n + 2)
                if ahead >= 1:
                    exp_1(n + 1)

            act.preload_act_table_set("natural_log_exp_and_others")
            act.wait_ge(s_feat, 32)
            act.wait_ge(s_init, 7)
            act.wait_ge(s_bias, 64)
            copy_feats(0)
            evac_featT(0)
            copy_feats(1)
            exp_1(0)
            step(0, first=True)
            with act.Fori(1, CHUNKS - 2) as n:
                step(n)
            step(CHUNKS - 2, ahead=1)
            step(CHUNKS - 1, ahead=0)

            def half_block(b, u, out_of=3):
                if out_of & 1:
                    act.wait_ge(aggT_ps, b + 1)
                    act.activation(aggT[u % 2][:, :], ps_aggT[u % 2][:, :], ACT.Copy).then_inc(aggT_sb, 1)
                if out_of & 4:
                    act.wait_ge(cap2, b - 1)
                    act.activation(soft2[u % 2][:, :], soft2[u % 2][:, :], ACT.Ln, bias=half[:, :], scale=0.5).then_inc(log2, 1)
                if out_of & 2:
                    act.wait_ge(z2_ps, b)
                    k = (u - 1) % 2
                    act.activation(soft2[k][:, :], ps_z2[k][:, :], ACT.Exp, bias=bo1[:, :]).then_inc(exp2, 1)

            for u in range(HGROUP):
                half_block(u, u, (1, 3)[u] if u < 2 else 7)
            with act.Fori(1, BGROUPS) as group:
                for u in range(HGROUP):
                    half_block(group * HGROUP + u, u, 7)
            half_block(HALVES, 0, 6)
            half_block(HALVES + 1, 1, 4)

        @block.tensor
        def _(pe):
            def transpose_feats(n):
                pe.wait_ge(feat_sb, n + 1)
                pe.transpose(ps_fT, feat_in[:, :], ident[:, :]).then_inc(fT_ps, 1)

            def filter_1(n, first=False):
                if not first:
                    pe.wait_ge(act1_sb, n)
                pe.wait_ge(fT_sb, n + 1)
                for i in range(TPC):
                    mm = pe.matmul(ps_a1[:, i::TPC], w1_at[:, i, :], featT[:, :], start=True, stop=True)
                mm.then_inc(a1_ps, 1)

            def rows_product(bank, lhs, w, parts):
                for j in range(TPC):
                    tile = bank[:, j * D : (j + 1) * D]
                    if parts is not None:
                        pe.matmul(tile, ones_bf[:, :], parts[:, :], start=True, stop=False)
                    mm = pe.matmul(tile, lhs[:, j * P : (j + 1) * P], w[:, :], start=parts is None, stop=True)
                return mm

            def filter_2(n, first=False):
                if not first:
                    pe.wait_ge(msg_sb, n)
                pe.wait_ge(act1_sb, n + 1)
                rows_product(ps_w, act1, w2, bias_parts[0]).then_inc(w_ps, 1)

            def transpose_h(n):
                pe.wait_ge(h_done, n + 1)
                for j in range(TPC):
                    tr = pe.transpose(ps_hT[:, j * P : (j + 1) * P], h[:, j * P : (j + 1) * P], ident[:, :])
                tr.then_inc(hT_ps, 1)

            def in2f(n, first=False):
                if not first:
                    pe.wait_ge(g_sb, n)
                pe.wait_ge(hT_sb, n + 1)
                rows_product(ps_g, hT, w_in, None).then_inc(g_ps, 1)

            def sum_pairs(n, first=False):
                if not first:
                    pe.wait_ge(msgs_ready, n)
                pe.wait_ge(pairs_sb, n + 1)
                pe.wait_ge(msg_sb, n + 1)
                for to in range(TPC):
                    for j in range(to + 1):
                        at = (to - j) * P
                        mm = pe.matmul(ps_sum[:, to * D : (to + 1) * D], pairs[j][:, at : at + P], msg[:, j * D : (j + 1) * D], start=j == 0, stop=j == to)
                mm.then_inc(sum_ps, 1)

            def step(n, first=False, second=False, ahead=True):
                if not first:
                    sum_pairs(n - 1, first=second)
                transpose_h(n)
                in2f(n, first)
                if ahead:
                    transpose_feats(n + 1)
                filter_2(n, first)
                if ahead:
                    filter_1(n + 1)

            pe.wait_ge(s_ident, 4)
            for k, rows in enumerate((dst_rows_f, src_rows_f, weight_rows)):
                if k < 2:
                    pe.wait_ge(s_prep, (1, 3)[k])
                else:
                    pe.wait_ge(s_wts, 32)
                for j in range(TPC):
                    tr = pe.transpose(bank[k][:, j * CHUNKS : (j + 1) * CHUNKS], rows[0:CHUNKS, j * P : (j + 1) * P], ident[0:CHUNKS, 0:CHUNKS])
                tr.then_inc(s_pprep, 1)
            pe.wait_ge(s_par, 16 * 8)
            pe.wait_ge(s_prep, 5)
            pe.wait_ge(s_iota, 2)
            transpose_feats(0)
            filter_1(0, first=True)
            step(0, first=True)
            step(1, second=True)
            with pe.Fori(2, CHUNKS - 1) as n:
                step(n)
            step(CHUNKS - 1, ahead=False)
            sum_pairs(CHUNKS - 1)

            def half_block(b, u, group, parts=7, early=False):
                if parts & 1:
                    k = u // 2
                    if u % 2 == 0:
                        pe.wait_ge(agg_in[k], group * 16 + 16)
                    for j in range(TPC):
                        at = (u % 2 * TPC + j) * D
                        tr = pe.transpose(ps_aggT[u % 2][:, j * P : (j + 1) * P], agg_in_sb[:, k, at : at + D], ident[:, :])
                    tr.then_inc(aggT_ps, 1)
                if parts & 4:
                    k = (u - 3) % 2
                    if not early:
                        pe.wait_ge(added, b - 4)
                    pe.wait_ge(act2_sb, b - 2)
                    rows_product(ps_o[k], act2[k], wo2, bias_parts[1]).then_inc(o_ps, 1)
                if parts & 2:
                    k = (u - 1) % 2
                    pe.wait_ge(aggT_sb, b)
                    pe.matmul(ps_z2[k][:, :], wo1[:, :], aggT[k][:, :], start=True, stop=True).then_inc(z2_ps, 1)

            pe.wait_ge(msgs_ready, CHUNKS)
            for u in range(HGROUP):
                half_block(u, u, 0, 1 if u < 1 else 3 if u < 3 else 7, early=u < 5)
            with pe.Fori(1, BGROUPS) as group:
                for u in range(HGROUP):
                    half_block(group * HGROUP + u, u, group)
            half_block(HALVES, 0, None, 6)
            half_block(HALVES + 1, 1, None, 4)
            half_block(HALVES + 2, 2, None, 4)

        @block.vector
        def _(dve):
            dve.memset(dst_rows, 0).then_inc(s_init, 1)
            dve.memset(src_rows, DUMP + CHUNK - 1).then_inc(s_init, 1)
            dve.memset(weight_rows[:, :], 0.0).then_inc(s_init, 1)
            dve.memset(w1_at[:, :, :], 0.0).then_inc(s_init, 1)
            dve.memset(feats[:, full, :], 0.0).then_inc(s_init, 1)
            dve.memset(zeros, 0.0).then_inc(s_init, 1)
            dve.memset(half[:, :], 0.5).then_inc(s_init, 1)
            mine = 0

            def own(instruction):
                nonlocal mine
                mine += 1
                instruction.then_inc(s_mine, 1)
                dve.wait_ge(s_mine, mine)

            def columns(table, bank):
                return dve.tensor_copy(table.rearrange("p (n j) -> p n j", j=TPC), bank[:, 0:TILES].rearrange("p (j n) -> p n j", j=TPC))

            dve.wait_ge(s_dst, 32)
            dve.tensor_copy(dst_rows_f[0:CHUNKS, :], dst_rows[0:CHUNKS, :]).then_inc(s_prep, 1)
            dve.wait_ge(s_pprep, 1)
            columns(dst_idx[:, :], bank[0]).then_inc(s_prep, 1)
            dve.wait_ge(s_src, 32)
            dve.tensor_copy(src_rows_f[0:CHUNKS, :], src_rows[0:CHUNKS, :]).then_inc(s_prep, 1)
            dve.wait_ge(s_ident, 4)
            own(dve.tensor_copy(ps_mask[:, :], later_mask))
            dve.wait_ge(s_iota, 1)
            own(dve.tensor_copy(dump_row[:, :], dump_i))
            dve.wait_ge(s_pprep, 3)
            own(columns(src_cols[:, 0, :], bank[1]))
            tiles = "p (n j) -> p n j"
            own(dve.tensor_tensor(
                src_cols[:, 1, :].rearrange(tiles, j=TPC), src_cols[:, 0, :].rearrange(tiles, j=TPC),
                dump_row[:, :].rearrange("p (a j) -> p a j", a=1).to_broadcast([P, CHUNKS, TPC]), ALU.subtract,
            ))
            own(dve.memset(per_edge[:, :, :], 0.0))
            columns(weight[:, :], bank[2]).then_inc(s_prep, 1)
            dve.wait_ge(s_bias, 64)
            own(dve.tensor_scalar(b1_ln2[:, :], b1[:, :], -LN2, None, ALU.add))
            own(dve.tensor_scalar(bo1_ln2[:, :], bo1[:, :], -LN2, None, ALU.add))
            for rows, parts in zip(bias_rows, bias_parts):
                own(dve.memset(parts[:, :], 0.0))
                for i in range(3):
                    own(dve.tensor_copy(bias_bf[i][:, :], rows[:, :]))
                    if i < 2:
                        own(dve.tensor_tensor(rows[:, :], rows[:, :], bias_bf[i][:, :], ALU.subtract))
                    own(dve.tensor_copy(parts[32 * i : 32 * i + 1, :], bias_bf[i][32 * i : 32 * i + 1, :]))
            dve.wait_ge(s_pad, 16)
            dve.wait_ge(s_prep, 4)
            dve.nop().then_inc(s_prep, 1)

            def stats_of(n, c, group):
                dve.wait_ge(gathered[c], 16 * TPC * (group + 1))
                for j in range(TPC):
                    bn = dve.bn_stats(stats[:, c * TPC + j, :], rows_io[:, tile_cols(n * TPC + j)])
                bn.then_inc(bn_done, 1)

            LN_STEPS = 12 + 3 * NEWTON

            def finish_stats(group):
                k = 0

                def then(instruction):
                    nonlocal k
                    k += 1
                    instruction.then_inc(ln_step, 1)
                    dve.wait_ge(ln_step, group * LN_STEPS + k)

                mean0, mean1, m20, m21 = (stats[:, :, i] for i in (1, 4, 2, 5))
                dve.wait_ge(bn_done, (group + 1) * GROUP)
                then(dve.tensor_tensor(mean[:, :], mean0, mean1, ALU.add))
                then(dve.tensor_tensor(ln_a[:, :], mean0, mean1, ALU.subtract))
                then(dve.tensor_tensor(var[:, :], m20, m21, ALU.add))
                then(dve.tensor_scalar(mean[:, :], mean[:, :], 0.5, None, ALU.mult))
                then(dve.scalar_tensor_tensor(ln_a[:, :], ln_a[:, :], 0.25, ln_a[:, :], ALU.mult, ALU.mult))
                then(dve.tensor_scalar(var[:, :], var[:, :], 1.0 / D, LN_EPS, ALU.mult, ALU.add))
                then(dve.tensor_tensor(var[:, :], var[:, :], ln_a[:, :], ALU.add))
                then(dve.tensor_single_scalar(ln_b[:, :].bitcast(I32), var[:, :].bitcast(I32), 1, ALU.logical_shift_right))
                then(dve.tensor_scalar(rsq[:, :].bitcast(I32), ln_b[:, :].bitcast(I32), -1.0, RSQRT_MAGIC, ALU.mult, ALU.add))
                for _ in range(NEWTON):
                    then(dve.tensor_tensor(ln_a[:, :], rsq[:, :], rsq[:, :], ALU.mult))
                    then(dve.scalar_tensor_tensor(ln_a[:, :], ln_a[:, :], -0.5, var[:, :], ALU.mult, ALU.mult))
                    then(dve.scalar_tensor_tensor(rsq[:, :], ln_a[:, :], 1.5, rsq[:, :], ALU.add, ALU.mult))
                then(dve.tensor_copy(per_edge[:, :, 0:TPC], per_edge[:, :, GT:]))
                then(dve.tensor_copy(per_edge[:, 1:3, TPC:], src_cols[:, :, bass.ds(group * GT, GT)]))
                then(dve.tensor_tensor(scale[:, TPC:], rsq[:, :], weight[:, bass.ds(group * GT, GT)], ALU.mult))
                assert k == LN_STEPS

            def find_pairs(n, c, group):
                before = group + 1 if c else group
                dve.wait_ge(src_in[(c - 1) % GROUP], before * 16)
                if not (isinstance(n, int) and n == 0):
                    dve.wait_ge(sum_ps, n)
                for j in range(TPC):
                    k = c * TPC + j
                    op = dve.scalar_tensor_tensor(
                        pairs[j][:, :], src_all[:, (c - 1) % GROUP, j * P :], src_now[:, k : k + 1], ps_mask[:, 0 : CHUNK - j * P],
                        ALU.is_equal, ALU.mult, accum_out=later[:, j : j + 1],
                    )
                op.then_inc(pairs_sb, 1)
                dve.wait_ge(pairs_sb, n + 1)
                dve.scalar_tensor_tensor(picked[:, :], later[:, :], 0.0, src_less_dump[:, c * TPC : (c + 1) * TPC], ALU.is_equal, ALU.mult).then_inc(picked_sb, 1)

            def set_rows(n):
                dve.wait_ge(picked_sb, n + 1)
                dve.tensor_tensor(agg_idx[:, bass.ds(n * TPC, TPC)], picked[:, :], dump_row[:, :], ALU.add)

            def messages(n, c):
                dve.wait_ge(w_ps, n + 1)
                dve.wait_ge(g_sb, n + 1)
                for j in range(TPC):
                    k, cols = c * TPC + j, slice(j * D, (j + 1) * D)
                    op = dve.scalar_tensor_tensor(msg[:, cols], ps_w[:, cols], scale[:, k : k + 1], g[:, cols], ALU.mult, ALU.mult)
                op.then_inc(msg_sb, 1)

            def centre(n, c):
                for j in range(TPC):
                    k = c * TPC + j
                    op = dve.tensor_scalar(h[:, j * P : (j + 1) * P], rows_io[:, tile_cols(n * TPC + j)], mean[:, k : k + 1], 0.0, ALU.subtract, ALU.max)
                op.then_inc(h_done, 1)

            def add_pairs(n):
                dve.wait_ge(sum_ps, n + 1)
                dve.wait_ge(msg_sb, n + 1)
                dve.tensor_tensor(rows_io[:, bass.ds(n * CHUNK, CHUNK)], ps_sum[:, :], msg[:, :], ALU.add).then_inc(msgs_ready, 1)

            def step(n, c, group, first=False, now=True, lead=True):
                if not first:
                    find_pairs(n - 1, c, group)
                    messages(n - 1, c)
                    set_rows(n - 1)
                if now:
                    if not first:
                        dve.wait_ge(hT_ps, n)
                    centre(n, c)
                    dve.wait_ge(exp1, n + 1)
                    dve.tensor_scalar(soft1[:, :], soft1[:, :], EXP_CAP, None, ALU.min).then_inc(cap1, 1)
                if lead:
                    stats_of(n + GROUP, c, group + 1)
                if now:
                    dve.wait_ge(log1, n + 1)
                    dve.scalar_tensor_tensor(act1[:, :], ps_a1[:, :], b1_ln2[:, :], soft1[:, :], ALU.add, ALU.max).then_inc(act1_sb, 1)
                if not first:
                    add_pairs(n - 1)

            for c in range(GROUP):
                stats_of(c, c, 0)
            finish_stats(0)
            for c in range(GROUP):
                step(c, c, 0, first=c == 0)
            finish_stats(1)
            with dve.Fori(1, GROUPS - 1) as group:
                for c in range(GROUP):
                    step(group * GROUP + c, c, group)
                finish_stats(group + 1)
            for c in range(GROUP):
                step((GROUPS - 1) * GROUP + c, c, GROUPS - 1, lead=False)
            step(CHUNKS, GROUP, GROUPS - 1, now=False, lead=False)

            def half_block(b, u, group, parts=7, early=False):
                if parts & 1:
                    if not early:
                        dve.wait_ge(o_ps, b - 3)
                    dve.wait_ge(log2, b - 1)
                    k = u % 2
                    dve.scalar_tensor_tensor(act2[k][:, :], ps_z2[k][:, :], bo1_ln2[:, :], soft2[k][:, :], ALU.add, ALU.max).then_inc(act2_sb, 1)
                if parts & 2:
                    dve.wait_ge(exp2, b)
                    k = (u - 1) % 2
                    dve.tensor_scalar(soft2[k][:, :], soft2[k][:, :], EXP_CAP, None, ALU.min).then_inc(cap2, 1)
                if parts & 4:
                    v = (u - 3) % HGROUP
                    if v % 2 == 0:
                        dve.wait_ge(x_in[v // 2], (group + 1 if u >= 3 else group) * 16)
                    dve.wait_ge(o_ps, b - 2)
                    rows = x_sb[:, v // 2, (v % 2) * CHUNK : (v % 2 + 1) * CHUNK]
                    dve.tensor_tensor(rows, ps_o[v % 2][:, :], rows, ALU.add).then_inc(added, 1)

            for u in range(1, HGROUP):
                half_block(u, u, 0, 2 if u < 2 else 3 if u < 3 else 7, early=u < 4)
            with dve.Fori(1, BGROUPS) as group:
                for u in range(HGROUP):
                    half_block(group * HGROUP + u, u, group)
            half_block(HALVES, 0, BGROUPS)
            half_block(HALVES + 1, 1, BGROUPS, 5)
            half_block(HALVES + 2, 2, BGROUPS, 4)


_INS = [
    "x", "src", "dst", "edge_attr_20", "edge_weight", "L0_gnn_W_in2f", "L0_gnn_W_f1", "L0_gnn_b_f1",
    "L0_gnn_W_f2", "L0_gnn_b_f2", "L0_gnn_W_o1", "L0_gnn_b_o1", "L0_gnn_W_o2", "L0_gnn_b_o2",
]


def kernel(**inputs):
    import numpy as _np
    import concourse.bacc as _bacc
    from concourse import mybir as _mybir
    from concourse.bass_utils import run_bass_kernel_spmd as _run

    nc = _bacc.Bacc("TRN2", target_bir_lowering=False, num_devices=1)
    arrays, args = {}, []
    for name in _INS:
        a = _np.ascontiguousarray(inputs[name])
        arrays[f"in_{name}_dram"] = a
        args.append(nc.dram_tensor(f"in_{name}_dram", a.shape, _mybir.dt.from_np(a.dtype), kind="ExternalInput").ap())
    args.append(nc.dram_tensor("out_0_dram", (NODES, D), F32, kind="ExternalOutput").ap())
    gnn_layer(nc, *args)
    r = _run(nc, [arrays], core_ids=[0])
    return r.results[0]["out_0_dram"]
```

```python
import math
from contextlib import ExitStack

import concourse.bass as bass
from concourse import mybir

F32 = mybir.dt.float32
BF16 = mybir.dt.bfloat16
I32 = mybir.dt.int32
ALU = mybir.AluOpType
ACT = mybir.ActivationFunctionType

P = 128
NODES = 100000
EDGES = 25000
D = 128
RBF = 20
LN_EPS = 1e-5
LN2 = math.log(2.0)
EXP_CAP = 2.0**60
RSQRT_MAGIC = float(0x5F3759DF)
NEWTON = 3

TPC = 4
CHUNK = TPC * P
CHUNKS = -(-EDGES // CHUNK)
TILES = CHUNKS * TPC
GROUP = 7
GROUPS = CHUNKS // GROUP
GT = GROUP * TPC
STATS_STEPS = 4
TAIL = EDGES - (CHUNKS - 1) * CHUNK

ZROWS = 2048
ZBLOCKS = -(-NODES // ZROWS)
DUMP = ZBLOCKS * ZROWS

CLEAR_GROUPS = 1 + (ZBLOCKS - GROUP) // (2 * GROUP)
assert GROUP + 2 * GROUP * (CLEAR_GROUPS - 1) == ZBLOCKS

ROWS = 1024
RPP = ROWS // P
BLOCK = RPP * D
BLOCKS = -(-NODES // ROWS)
HALVES = 2 * BLOCKS
SLOTS = 7
LAG = 2
BGROUP = SLOTS
BGROUPS = BLOCKS // BGROUP
HGROUP = 2 * BGROUP

assert NEWTON == GROUP - STATS_STEPS and 2 * STATS_STEPS >= GROUP
assert CHUNKS == GROUP * GROUPS and BLOCKS == BGROUP * BGROUPS and ROWS == 2 * TPC * P


def gnn_layer(nc, x, src, dst, edge_attr, edge_weight, w_in2f, w_f1, b_f1, w_f2, b_f2, w_o1, b_o1, w_o2, b_o2, out):
    agg = nc.dram_tensor("agg", (DUMP + CHUNK, D), F32, kind="Internal").ap()
    src_padded = nc.dram_tensor("src_padded", (CHUNKS, CHUNK), I32, kind="Internal").ap()

    with ExitStack() as ctx:

        def sb(name, shape, dt=F32):
            return ctx.enter_context(nc.sbuf_tensor(name, shape, dt))

        def ps(name):
            return ctx.enter_context(nc.psum_tensor(name, [P, CHUNK], F32))

        def sem(name):
            return ctx.enter_context(nc.semaphore(name))

        rows_io = sb("rows_io", [P, TILES * D])
        agg_in_sb = rows_io[:, 0 : SLOTS * BLOCK].rearrange("p (k f) -> p k f", k=SLOTS)
        x_sb = sb("x_sb", [P, SLOTS, BLOCK])
        feats = sb("feats", [P, CHUNKS, TPC * RBF])
        src_all = sb("src_all", [P, GROUP, CHUNK], I32)
        dst_idx = sb("dst_idx", [P, TILES], I32)
        agg_idx = sb("agg_idx", [P, TILES], I32)
        src_cols = sb("src_cols", [P, 2, TILES])
        weight = sb("weight", [P, TILES])
        dump_row = sb("dump_row", [P, TPC])
        dump_row_1 = sb("dump_row_1", [P, TPC])
        stats = sb("stats", [P, GT, 6])
        mean = sb("mean", [P, GT])
        mean_2 = sb("mean_2", [P, GT])
        per_edge = sb("per_edge", [P, 3, GT])
        src_now, src_less_dump, scale = (per_edge[:, i, :] for i in range(3))
        count = sb("count", [P, TPC])
        again = sb("again", [P, TPC])
        last = sb("last", [P, 2, TPC])
        last_before = sb("last_before", [P, 2, TPC])
        last_bf = sb("last_bf", [P, TPC], BF16)
        picked = sb("picked", [P, TPC])
        var = sb("var", [P, GT])
        ln_a = sb("ln_a", [P, GT])
        ln_b = sb("ln_b", [P, GT])
        rsq = sb("rsq", [P, GT])
        h = sb("h", [P, CHUNK])
        hT = sb("hT", [P, CHUNK])
        g = sb("g", [P, CHUNK])
        feat_in = sb("feat_in", [P, TPC * RBF])
        featT = sb("featT", [TPC * RBF, P])
        soft1 = sb("soft1", [P, CHUNK])
        act1 = sb("act1", [P, CHUNK])
        msg = sb("msg", [P, CHUNK])
        pairs = [sb(f"pairs{j}", [P, CHUNK - j * P]) for j in range(TPC)]
        aggT = [sb(f"aggT{k}", [P, CHUNK]) for k in range(2)]
        soft2 = [sb(f"soft2{k}", [P, CHUNK]) for k in range(2)]
        act2 = [sb(f"act2{k}", [P, CHUNK]) for k in range(2)]
        onward = [None, aggT[0][:, 0:P], aggT[0][:, P : 3 * P], aggT[1][:, 0 : 3 * P]]
        ident = sb("ident", [P, P])
        ident_bf = sb("ident_bf", [P, P], BF16)
        ones_bf = sb("ones_bf", [P, P], BF16)
        w_in = sb("w_in", [P, D])
        w1_at = sb("w1_at", [TPC * RBF, TPC, D])
        w2 = sb("w2", [P, D])
        wo1 = sb("wo1", [P, D])
        wo2 = sb("wo2", [P, D])
        half = sb("half", [P, 1])
        b1 = sb("b1", [P, 1])
        bo1 = sb("bo1", [P, 1])
        b1_ln2 = sb("b1_ln2", [P, 1])
        bo1_ln2 = sb("bo1_ln2", [P, 1])
        b2_rows = sb("b2_rows", [P, D])
        bo2_rows = sb("bo2_rows", [P, D])
        b2_bf = [sb(f"b2_bf{i}", [P, D], BF16) for i in range(3)]
        b2_parts = sb("b2_parts", [P, TPC, D], BF16)

        dst_rows = hT[:, :].bitcast(I32)
        dst_rows_f = g
        src_rows = act1[:, :].bitcast(I32)
        src_rows_f = soft1
        weight_rows = msg
        zeros = x_sb[:, 0:2, :]
        pair_mask = x_sb[:, 2, 0:CHUNK]
        dump_i = x_sb[:, 3, 0:TPC].bitcast(I32)

        bank = [ps(f"bank{k}") for k in range(7)]
        ps_mask = ps("ps_mask")
        ps_hT, ps_g, ps_a1, ps_w, ps_sum, ps_last = bank[0:6]
        ps_fT = bank[6][0 : TPC * RBF, 0:P]
        ps_aggT, ps_z2, ps_o = bank[0:2], bank[2:4], bank[4:6]

        seen = sem("seen")
        s_mine = sem("s_mine")
        s_init = sem("s_init")
        s_dst = sem("s_dst")
        s_src = sem("s_src")
        s_pad = sem("s_pad")
        s_wts = sem("s_wts")
        s_par = sem("s_par")
        s_bias = sem("s_bias")
        s_feat = sem("s_feat")
        s_zero = sem("s_zero")
        s_ident = sem("s_ident")
        s_iota = sem("s_iota")
        s_prep = sem("s_prep")
        s_pprep = sem("s_pprep")
        agg_done = sem("agg_done")
        gathered = [sem(f"gathered{c}") for c in range(GROUP)]
        scattered = [sem(f"scattered{j}") for j in range(TPC)]
        src_in = [sem(f"src_in{c}") for c in range(GROUP)]
        x_in = [sem(f"x_in{k}") for k in range(SLOTS)]
        agg_in = [sem(f"agg_in{k}") for k in range(SLOTS)]
        stored = [sem(f"stored{k}") for k in range(SLOTS)]
        bn_done = sem("bn_done")
        ln_step = sem("ln_step")
        h_done = sem("h_done")
        hT_ps = sem("hT_ps")
        hT_sb = sem("hT_sb")
        g_ps = sem("g_ps")
        g_sb = sem("g_sb")
        feat_sb = sem("feat_sb")
        fT_ps = sem("fT_ps")
        fT_sb = sem("fT_sb")
        a1_ps = sem("a1_ps")
        exp1 = sem("exp1")
        cap1 = sem("cap1")
        log1 = sem("log1")
        act1_sb = sem("act1_sb")
        w_ps = sem("w_ps")
        pairs_sb = sem("pairs_sb")
        last_sb = sem("last_sb")
        last_ps = sem("last_ps")
        onward_sb = sem("onward_sb")
        picked_sb = sem("picked_sb")
        chosen = sem("chosen")
        rows_set = sem("rows_set")
        msg_sb = sem("msg_sb")
        paired = sem("paired")
        sum_ps = sem("sum_ps")
        msgs_ready = sem("msgs_ready")
        aggT_ps = sem("aggT_ps")
        aggT_sb = sem("aggT_sb")
        z2_ps = sem("z2_ps")
        exp2 = sem("exp2")
        cap2 = sem("cap2")
        log2 = sem("log2")
        act2_sb = sem("act2_sb")
        o_ps = sem("o_ps")
        added = sem("added")
        biased = sem("biased")

        block = ctx.enter_context(nc.Block())

        def tile_cols(t):
            return bass.ds(t * D, D)

        def block_rows(ap, m):
            at = min(m * ROWS, NODES - ROWS) if isinstance(m, int) else m * ROWS
            return ap[bass.ds(at, ROWS), :].rearrange("(p r) d -> p (r d)", p=P)

        full = CHUNKS - 1
        full_edges = full * CHUNK

        @block.sync
        def _(sp):
            def load_rows(tile, v, s):
                sp.dma_start(tile[0:full, :], v[0:full_edges].rearrange("(n i) -> n i", i=CHUNK)).then_inc(s, 16)
                sp.dma_start(tile[full:CHUNKS, 0:TAIL], v[full_edges:EDGES].rearrange("(n i) -> n i", n=1)).then_inc(s, 16)

            sp.wait_ge(s_init, 1)
            load_rows(dst_rows, dst, s_dst)
            sp.wait_ge(s_init, 2)
            load_rows(src_rows, src, s_src)
            sp.wait_ge(s_init, 3)
            load_rows(weight_rows, edge_weight, s_wts)
            for tile, v in ((b1, b_f1), (bo1, b_o1)):
                sp.dma_start(tile[:, :], v.rearrange("(p a) -> p a", a=1)).then_inc(s_bias, 16)
            for tile, v in ((b2_rows, b_f2), (bo2_rows, b_o2)):
                sp.dma_start(tile[:, :], v.rearrange("(a d) -> a d", a=1).to_broadcast([P, D])).then_inc(s_bias, 16)
            for tile, v in ((w_in, w_in2f), (w2, w_f2), (wo1, w_o1), (wo2, w_o2)):
                sp.dma_start(tile[:, :], v[:, :]).then_inc(s_par, 16)
            sp.wait_ge(s_init, 5)
            for i in range(TPC):
                sp.dma_start(w1_at[i * RBF : (i + 1) * RBF, i, :], w_f1[:, :]).then_inc(s_par, 16)
            by_quad = edge_attr[0:full_edges, :].rearrange("(n q i) k -> q n (i k)", q=P, i=TPC)
            sp.dma_start(feats[:, 0:full, :], by_quad).then_inc(s_feat, 16)
            sp.dma_start(feats[0 : TAIL // TPC, full, :], edge_attr[full_edges:EDGES, :].rearrange("(q i) k -> q (i k)", i=TPC)).then_inc(s_feat, 16)
            sp.wait_ge(s_prep, 4)
            sp.dma_start(src_padded[:, :], src_rows[0:CHUNKS, :]).then_inc(s_pad, 16)
            sp.wait_ge(s_pad, 16)

            def load_src(n, c):
                sp.dma_start(src_all[:, c, :], src_padded[bass.ds(n, 1), :].to_broadcast([P, CHUNK])).then_inc(src_in[c], 16)

            for c in range(GROUP):
                load_src(c, c)
            sp.wait_ge(s_init, 6)

            def clear(zb):
                sp.dma_start(agg[bass.ds(zb * ZROWS, ZROWS), :].rearrange("(p r) d -> p (r d)", p=P), zeros).then_inc(s_zero, 16)

            dump = agg[DUMP : DUMP + CHUNK, :].rearrange("(p r) d -> p (r d)", p=P)
            sp.dma_start(dump, x_sb[:, 0, 0:CHUNK]).then_inc(s_zero, 16)
            for zb in range(GROUP):
                clear(zb)

            def next_src(group, clears):
                for c in range(GROUP):
                    n = group * GROUP + c
                    sp.wait_ge(onward_sb, n - GROUP + 1)
                    load_src(n, c)
                    for i in range(clears):
                        clear(n * clears - GROUP * (clears - 1) + i)

            with sp.Fori(1, CLEAR_GROUPS) as group:
                next_src(group, 2)
            with sp.Fori(CLEAR_GROUPS, GROUPS) as group:
                next_src(group, 0)

            def load_x(m, k):
                sp.dma_start(x_sb[:, k, :], block_rows(x, m)).then_inc(x_in[k], 16)

            def load_agg(m, k):
                sp.dma_start(agg_in_sb[:, k, :], block_rows(agg, m)).then_inc(agg_in[k], 16)

            sp.wait_ge(s_zero, 16 * (ZBLOCKS + 1))
            sp.wait_ge(s_prep, 6)
            for m in range(SLOTS - LAG):
                load_x(m, m)
            sp.wait_ge(agg_done, 1)
            for m in range(SLOTS - LAG):
                load_agg(m, m)

            def turn(group, first=False, last=False):
                for k in range(BGROUP):
                    m = group * BGROUP + k
                    sp.wait_ge(added, 2 * m + 2)
                    if last and k == BGROUP - 1:
                        sp.wait_ge(stored[k - 1], 16 * BGROUPS)
                    sp.dma_start(block_rows(out, m), x_sb[:, k, :]).then_inc(stored[k], 16)
                    back = k - LAG
                    if back >= 0:
                        sp.wait_ge(stored[back], group * 16 + 16)
                    elif not first:
                        sp.wait_ge(stored[back % BGROUP], group * 16)
                    if not (last and back >= 0):
                        load_x(m + SLOTS - LAG, back % BGROUP)
                        load_agg(m + SLOTS - LAG, back % BGROUP)

            turn(0, first=True)
            with sp.Fori(1, BGROUPS - 1) as group:
                turn(group)
            turn(BGROUPS - 1, last=True)
            for k in range(BGROUP - LAG, BGROUP):
                sp.wait_ge(stored[k], 16 * BGROUPS)

        @block.gpsimd
        def _(gp):
            gp.memset(ident[:, :], 0.0).then_inc(s_ident, 1)
            gp.memset(pair_mask, 0.0).then_inc(s_ident, 1)
            gp.memset(ident_bf[:, :], 0.0).then_inc(s_ident, 1)
            gp.wait_ge(s_ident, 3)
            gp.affine_select(out=ident_bf[:, :], in_=ident_bf[:, :], compare_op=ALU.not_equal, fill=1.0, base=0, pattern=[[-1, P]], channel_multiplier=1).then_inc(s_ident, 1)
            gp.affine_select(out=ident[:, :], in_=ident[:, :], compare_op=ALU.not_equal, fill=1.0, base=0, pattern=[[-1, P]], channel_multiplier=1).then_inc(s_ident, 1)
            gp.affine_select(out=pair_mask, in_=pair_mask, compare_op=ALU.is_ge, fill=1.0, base=-1, pattern=[[-1, CHUNK]], channel_multiplier=1).then_inc(s_ident, 1)
            gp.iota(dump_i, pattern=[[P, TPC]], base=DUMP, channel_multiplier=1).then_inc(s_iota, 1)
            gp.memset(ones_bf[:, :], 1.0).then_inc(s_iota, 1)

            gp.wait_ge(s_prep, 2)
            for t in range(TILES):
                chunk = t // TPC
                c = chunk % GROUP
                if t % TPC == 0 and chunk >= GROUP:
                    gp.wait_ge(gathered[c], 16 * TPC * (chunk // GROUP))
                gp.indirect_dma_start(
                    rows_io[:, t * D : (t + 1) * D], None, x[:, :], bass.IndirectOffsetOnAxis(dst_idx[:, t : t + 1], 0)
                ).then_inc(gathered[c], 16)

            gp.wait_ge(s_zero, 16 * (ZBLOCKS + 1))
            for t in range(TILES):
                chunk, j = divmod(t, TPC)
                if j == 0:
                    gp.wait_ge(msgs_ready, chunk + 1)
                    gp.wait_ge(rows_set, chunk + 1)
                if chunk:
                    gp.wait_ge(scattered[j], 16 * chunk)
                gp.indirect_dma_start(
                    agg[:, :], bass.IndirectOffsetOnAxis(agg_idx[:, t : t + 1], 0), rows_io[:, t * D : (t + 1) * D], None, compute_op=ALU.add
                ).then_inc(scattered[j], 16)
            for j in range(TPC):
                gp.wait_ge(scattered[j], 16 * CHUNKS)
            gp.sem_inc(agg_done, 1)

            with gp.Fori(0, BGROUPS) as group:
                for k in range(BGROUP):
                    gp.wait_ge(x_in[k], group * 16 + 16)
                    rows = x_sb[:, k, :].rearrange("p (r d) -> p r d", d=D)
                    gp.tensor_tensor(rows, rows, bo2_rows[:, :].rearrange("p (a d) -> p a d", a=1).to_broadcast([P, RPP, D]), ALU.add).then_inc(biased, 1)

        @block.scalar
        def _(act):
            def copy_feats(n):
                act.activation(feat_in[:, :], feats[:, bass.ds(n, 1), :].rearrange("q n k -> q (n k)"), ACT.Copy).then_inc(feat_sb, 1)

            def evac_featT(n):
                act.wait_ge(fT_ps, n + 1)
                act.activation(featT[:, :], ps_fT, ACT.Copy).then_inc(fT_sb, 1)

            def exp_1(n):
                act.wait_ge(a1_ps, n + 1)
                act.activation(soft1[:, :], ps_a1[:, :], ACT.Exp, bias=b1[:, :]).then_inc(exp1, 1)

            def log_1(n):
                act.wait_ge(cap1, n + 1)
                act.activation(soft1[:, :], soft1[:, :], ACT.Ln, bias=half[:, :], scale=0.5).then_inc(log1, 1)

            def evac_hT(n):
                act.wait_ge(hT_ps, n + 1)
                act.activation(hT[:, :], ps_hT[:, :], ACT.Copy).then_inc(hT_sb, 1)

            def evac_g(n, first=False):
                if not first:
                    act.wait_ge(msg_sb, n)
                act.wait_ge(g_ps, n + 1)
                act.activation(g[:, :], ps_g[:, :], ACT.Copy).then_inc(g_sb, 1)

            def evac_sum(n):
                act.wait_ge(sum_ps, n + 1)
                act.sem_inc(seen, 1)
                act.activation(rows_io[:, bass.ds(n * CHUNK, CHUNK)], ps_sum[:, :], ACT.Copy).then_inc(msgs_ready, 1)

            def step(n, first=False, ahead=2):
                log_1(n)
                evac_hT(n)
                if ahead >= 1:
                    evac_featT(n + 1)
                if ahead >= 2:
                    copy_feats(n + 2)
                if not first:
                    evac_sum(n - 1)
                evac_g(n, first)
                if ahead >= 1:
                    exp_1(n + 1)

            act.preload_act_table_set("natural_log_exp_and_others")
            act.wait_ge(s_feat, 32)
            act.wait_ge(s_init, 7)
            act.wait_ge(s_bias, 64)
            copy_feats(0)
            evac_featT(0)
            copy_feats(1)
            exp_1(0)
            step(0, first=True)
            with act.Fori(1, CHUNKS - 2) as n:
                step(n)
            step(CHUNKS - 2, ahead=1)
            step(CHUNKS - 1, ahead=0)
            evac_sum(CHUNKS - 1)

            def half_block(b, u, out_of=3):
                if out_of & 4:
                    act.wait_ge(cap2, b - 1)
                    act.activation(soft2[u % 2][:, :], soft2[u % 2][:, :], ACT.Ln, bias=half[:, :], scale=0.5).then_inc(log2, 1)
                if out_of & 1:
                    act.wait_ge(aggT_ps, b + 1)
                    act.activation(aggT[u % 2][:, :], ps_aggT[u % 2][:, :], ACT.Copy).then_inc(aggT_sb, 1)
                if out_of & 2:
                    act.wait_ge(z2_ps, b)
                    k = (u - 1) % 2
                    act.activation(soft2[k][:, :], ps_z2[k][:, :], ACT.Exp, bias=bo1[:, :]).then_inc(exp2, 1)

            for u in range(HGROUP):
                half_block(u, u, (1, 3)[u] if u < 2 else 7)
            with act.Fori(1, BGROUPS) as group:
                for u in range(HGROUP):
                    half_block(group * HGROUP + u, u, 7)
            half_block(HALVES, 0, 6)
            half_block(HALVES + 1, 1, 4)

        @block.tensor
        def _(pe):
            def transpose_feats(n):
                pe.wait_ge(feat_sb, n + 1)
                pe.transpose(ps_fT, feat_in[:, :], ident[:, :]).then_inc(fT_ps, 1)

            def filter_1(n, first=False):
                if not first:
                    pe.wait_ge(act1_sb, n)
                pe.wait_ge(fT_sb, n + 1)
                for i in range(TPC):
                    mm = pe.matmul(ps_a1[:, i::TPC], w1_at[:, i, :], featT[:, :], start=True, stop=True)
                mm.then_inc(a1_ps, 1)

            def rows_product(bank, lhs, w, parts=None):
                if parts is not None:
                    pe.matmul(bank[:, :], ones_bf[:, :], parts, start=True, stop=True)
                for j in range(TPC):
                    tile = bank[:, j * D : (j + 1) * D]
                    mm = pe.matmul(tile, lhs[:, j * P : (j + 1) * P], w[:, :], start=parts is None, stop=True, skip_group_check=parts is not None)
                return mm

            def filter_2(n, first=False):
                if not first:
                    pe.wait_ge(msg_sb, n)
                pe.wait_ge(act1_sb, n + 1)
                rows_product(ps_w, act1, w2, b2_parts[:, :, :].rearrange("p j d -> p (j d)")).then_inc(w_ps, 1)

            def transpose_h(n):
                pe.wait_ge(h_done, n + 1)
                for j in range(TPC):
                    tr = pe.transpose(ps_hT[:, j * P : (j + 1) * P], h[:, j * P : (j + 1) * P], ident[:, :])
                tr.then_inc(hT_ps, 1)

            def in2f(n, first=False):
                if not first:
                    pe.wait_ge(g_sb, n)
                pe.wait_ge(hT_sb, n + 1)
                rows_product(ps_g, hT, w_in).then_inc(g_ps, 1)

            def sum_pairs(n, first=False):
                if not first:
                    pe.wait_ge(msgs_ready, n)
                pe.wait_ge(pairs_sb, n + 1)
                pe.wait_ge(msg_sb, n + 1)
                for to in range(TPC):
                    for j in range(to + 1):
                        at = (to - j) * P
                        mm = pe.matmul(
                            ps_sum[:, to * D : (to + 1) * D], pairs[j][:, at : at + P], msg[:, j * D : (j + 1) * D],
                            start=to == 0, stop=True, skip_group_check=True,
                        )
                mm.then_inc(paired, 1)
                if first:
                    pe.nop().then_inc(sum_ps, 1)

            def sum_onward(n):
                pe.wait_ge(onward_sb, n)
                for to in range(TPC - 1):
                    for i in range(to + 1, TPC):
                        sent = rows_io[:, bass.ds((n - 1) * CHUNK + i * D, D)]
                        mm = pe.matmul(ps_sum[:, to * D : (to + 1) * D], onward[i][:, to * P : (to + 1) * P], sent, start=False, stop=True, skip_group_check=True)
                mm.then_inc(sum_ps, 1)

            def spread_last(n):
                pe.wait_ge(last_sb, n + 1)
                for j in range(TPC - 1):
                    mm = pe.matmul(ps_last[:, j * P : (j + 1) * P], last_bf[:, j : j + 1].to_broadcast([P, P]), ident_bf[:, :], start=True, stop=True)
                mm.then_inc(last_ps, 1)

            def step(n, first=False, second=False, ahead=True):
                if not first:
                    sum_pairs(n - 1, first=second)
                transpose_h(n)
                if ahead:
                    transpose_feats(n + 1)
                if not first and not second:
                    sum_onward(n - 1)
                in2f(n, first)
                filter_2(n, first)
                if not first:
                    spread_last(n)
                if ahead:
                    filter_1(n + 1)

            pe.wait_ge(s_ident, 6)
            for k, rows in enumerate((dst_rows_f, src_rows_f, weight_rows)):
                if k < 2:
                    pe.wait_ge(s_prep, (1, 3)[k])
                else:
                    pe.wait_ge(s_wts, 32)
                for j in range(TPC):
                    tr = pe.transpose(bank[k][:, j * CHUNKS : (j + 1) * CHUNKS], rows[0:CHUNKS, j * P : (j + 1) * P], ident[0:CHUNKS, 0:CHUNKS])
                tr.then_inc(s_pprep, 1)
            pe.wait_ge(s_par, 16 * 8)
            pe.wait_ge(s_prep, 6)
            pe.wait_ge(s_iota, 2)
            transpose_feats(0)
            filter_1(0, first=True)
            step(0, first=True)
            step(1, second=True)
            with pe.Fori(2, CHUNKS - 1) as n:
                step(n)
            step(CHUNKS - 1, ahead=False)
            sum_pairs(CHUNKS - 1)
            sum_onward(CHUNKS - 1)

            def half_block(b, u, group, parts=7, early=False, first=False):
                if parts & 1:
                    k = u // 2
                    if u % 2 == 0:
                        pe.wait_ge(agg_in[k], group * 16 + 16)
                    for j in range(TPC):
                        at = (u % 2 * TPC + j) * D
                        tr = pe.transpose(ps_aggT[u % 2][:, j * P : (j + 1) * P], agg_in_sb[:, k, at : at + D], ident[:, :])
                    tr.then_inc(aggT_ps, 1)
                if parts & 2:
                    k = (u - 1) % 2
                    if not first:
                        pe.wait_ge(act2_sb, b - 2)
                    pe.wait_ge(aggT_sb, b)
                    pe.matmul(ps_z2[k][:, :], wo1[:, :], aggT[k][:, :], start=True, stop=True).then_inc(z2_ps, 1)
                if parts & 4:
                    k = (u - 3) % 2
                    if not early:
                        pe.wait_ge(added, b - 4)
                    pe.wait_ge(act2_sb, b - 2)
                    rows_product(ps_o[k], act2[k], wo2).then_inc(o_ps, 1)

            pe.wait_ge(msgs_ready, CHUNKS)
            for u in range(HGROUP):
                half_block(u, u, 0, 1 if u < 1 else 3 if u < 3 else 7, early=u < 5, first=u < 3)
            with pe.Fori(1, BGROUPS) as group:
                for u in range(HGROUP):
                    half_block(group * HGROUP + u, u, group)
            half_block(HALVES, 0, None, 6)
            half_block(HALVES + 1, 1, None, 4)
            half_block(HALVES + 2, 2, None, 4)

        @block.vector
        def _(dve):
            dve.memset(dst_rows, 0).then_inc(s_init, 1)
            dve.memset(src_rows, DUMP + CHUNK - 1).then_inc(s_init, 1)
            dve.memset(weight_rows[:, :], 0.0).then_inc(s_init, 1)
            dve.memset(w1_at[:, :, :], 0.0).then_inc(s_init, 1)
            dve.memset(feats[:, full, :], 0.0).then_inc(s_init, 1)
            dve.memset(zeros, 0.0).then_inc(s_init, 1)
            dve.memset(half[:, :], 0.5).then_inc(s_init, 1)
            mine = 0

            def own(instruction):
                nonlocal mine
                mine += 1
                instruction.then_inc(s_mine, 1)
                dve.wait_ge(s_mine, mine)

            def columns(table, bank):
                return dve.tensor_copy(table.rearrange("p (n j) -> p n j", j=TPC), bank[:, 0:TILES].rearrange("p (j n) -> p n j", j=TPC))

            dve.wait_ge(s_dst, 32)
            dve.tensor_copy(dst_rows_f[0:CHUNKS, :], dst_rows[0:CHUNKS, :]).then_inc(s_prep, 1)
            dve.wait_ge(s_pprep, 1)
            columns(dst_idx[:, :], bank[0]).then_inc(s_prep, 1)
            dve.wait_ge(s_src, 32)
            dve.tensor_scalar(src_rows_f[0:CHUNKS, :], src_rows[0:CHUNKS, :], 1.0, None, ALU.add).then_inc(s_prep, 1)
            dve.wait_ge(s_prep, 3)
            dve.tensor_copy(src_rows[0:CHUNKS, :], src_rows_f[0:CHUNKS, :]).then_inc(s_prep, 1)
            dve.wait_ge(s_ident, 6)
            own(dve.tensor_copy(ps_mask[:, :], pair_mask))
            dve.wait_ge(s_iota, 1)
            own(dve.tensor_copy(dump_row[:, :], dump_i))
            own(dve.tensor_scalar(dump_row_1[:, :], dump_row[:, :], 1.0, None, ALU.add))
            dve.wait_ge(s_pprep, 3)
            own(columns(src_cols[:, 0, :], bank[1]))
            tiles = "p (n j) -> p n j"
            own(dve.tensor_tensor(
                src_cols[:, 1, :].rearrange(tiles, j=TPC), src_cols[:, 0, :].rearrange(tiles, j=TPC),
                dump_row_1[:, :].rearrange("p (a j) -> p a j", a=1).to_broadcast([P, CHUNKS, TPC]), ALU.subtract,
            ))
            columns(weight[:, :], bank[2]).then_inc(s_prep, 1)
            dve.wait_ge(s_bias, 64)
            own(dve.tensor_scalar(b1_ln2[:, :], b1[:, :], -LN2, None, ALU.add))
            own(dve.tensor_scalar(bo1_ln2[:, :], bo1[:, :], -LN2, None, ALU.add))
            own(dve.memset(b2_parts[:, :, :], 0.0))
            for i in range(3):
                own(dve.tensor_copy(b2_bf[i][:, :], b2_rows[:, :]))
                if i < 2:
                    own(dve.tensor_tensor(b2_rows[:, :], b2_rows[:, :], b2_bf[i][:, :], ALU.subtract))
                one = slice(32 * i, 32 * i + 1)
                own(dve.tensor_copy(b2_parts[one, :, :], b2_bf[i][one, :].rearrange("p (a d) -> p a d", a=1).to_broadcast([1, TPC, D])))
            own(dve.memset(again[:, :], 0.0))
            dve.wait_ge(s_pad, 16)
            dve.wait_ge(s_prep, 5)
            dve.nop().then_inc(s_prep, 1)

            def stats_of(n, c, group):
                dve.wait_ge(gathered[c], 16 * TPC * (group + 1))
                for j in range(TPC):
                    bn = dve.bn_stats(stats[:, c * TPC + j, :], rows_io[:, tile_cols(n * TPC + j)])
                bn.then_inc(bn_done, 1)

            LN_STEPS = 6 + 3 * NEWTON

            def finish_stats(group, part):
                k = 0

                def settle(instruction):
                    nonlocal k
                    k += 1
                    instruction.then_inc(ln_step, 1)
                    dve.wait_ge(ln_step, group * LN_STEPS + k)

                def newton():
                    settle(dve.tensor_tensor(ln_a[:, :], rsq[:, :], rsq[:, :], ALU.mult))
                    settle(dve.scalar_tensor_tensor(ln_a[:, :], ln_a[:, :], -0.5, var[:, :], ALU.mult, ALU.mult))
                    settle(dve.scalar_tensor_tensor(rsq[:, :], ln_a[:, :], 1.5, rsq[:, :], ALU.add, ALU.mult))

                if part == 0:
                    mean0, mean1, m20, m21 = (stats[:, :, i] for i in (1, 4, 2, 5))
                    dve.wait_ge(bn_done, (group + 1) * GROUP)
                    dve.tensor_tensor(var[:, :], m20, m21, ALU.add)
                    dve.tensor_tensor(mean_2[:, :], mean0, mean1, ALU.add)
                    settle(dve.tensor_tensor(ln_a[:, :], mean0, mean1, ALU.subtract))
                    dve.tensor_scalar(var[:, :], var[:, :], 1.0 / D, LN_EPS, ALU.mult, ALU.add)
                    settle(dve.scalar_tensor_tensor(ln_a[:, :], ln_a[:, :], 0.25, ln_a[:, :], ALU.mult, ALU.mult))
                    settle(dve.tensor_tensor(var[:, :], var[:, :], ln_a[:, :], ALU.add))
                    settle(dve.tensor_single_scalar(ln_b[:, :].bitcast(I32), var[:, :].bitcast(I32), 1, ALU.logical_shift_right))
                    settle(dve.tensor_scalar(rsq[:, :].bitcast(I32), ln_b[:, :].bitcast(I32), -1.0, RSQRT_MAGIC, ALU.mult, ALU.add))
                else:
                    k = 5 + 3 * (part - 1)
                    newton()

            def enter_group(group):
                tiles_of = bass.ds(group * GT, GT)
                dve.tensor_copy(per_edge[:, 0:2, :], src_cols[:, :, tiles_of])
                dve.tensor_tensor(scale, rsq[:, :], weight[:, tiles_of], ALU.mult)
                dve.tensor_scalar(mean[:, :], mean_2[:, :], 0.5, None, ALU.mult).then_inc(ln_step, 1)
                dve.wait_ge(ln_step, (group + 1) * LN_STEPS)

            def find_pairs(n, c, group, first=False):
                dve.wait_ge(src_in[c], group * 16 + 16)
                if not first:
                    dve.tensor_copy(last_before[:, :, :], last[:, :, :])
                    dve.wait_ge(paired, n)
                for j in range(TPC):
                    k = c * TPC + j
                    op = dve.scalar_tensor_tensor(
                        pairs[j][:, :], src_all[:, c, j * P :], src_now[:, k : k + 1], ps_mask[:, 0 : CHUNK - j * P],
                        ALU.is_equal, ALU.mult, accum_out=count[:, j : j + 1],
                    )
                op.then_inc(pairs_sb, 1)
                dve.wait_ge(pairs_sb, n + 1)
                now = slice(c * TPC, (c + 1) * TPC)
                twice = count[:, :].rearrange("p (a j) -> p a j", a=1).to_broadcast([P, 2, TPC])
                dve.tensor_scalar(last_bf[:, :], count[:, :], 1.0, None, ALU.is_equal).then_inc(last_sb, 1)
                dve.scalar_tensor_tensor(last[:, :, :], twice, 1.0, per_edge[:, 0:2, now], ALU.is_equal, ALU.mult).then_inc(picked_sb, 1)

            def find_onward(n, c):
                dve.wait_ge(last_ps, n + 1)
                dve.wait_ge(picked_sb, n + 2)
                dve.wait_ge(sum_ps, n + 1)
                for i in range(1, TPC):
                    op = dve.scalar_tensor_tensor(
                        onward[i], src_all[:, c, 0 : i * P], last_before[:, 0, i : i + 1], ps_last[:, 0 : i * P],
                        ALU.is_equal, ALU.mult, accum_out=again[:, i : i + 1],
                    )
                op.then_inc(onward_sb, 1)
                dve.wait_ge(onward_sb, n + 1)
                set_rows(n, last_before[:, 1, :])

            def set_rows(n, of_last):
                dve.scalar_tensor_tensor(picked[:, :], again[:, :], 0.0, of_last, ALU.is_equal, ALU.mult).then_inc(chosen, 1)
                dve.wait_ge(chosen, n + 1)
                dve.tensor_tensor(agg_idx[:, bass.ds(n * TPC, TPC)], picked[:, :], dump_row[:, :], ALU.add).then_inc(rows_set, 1)

            def messages(n, c):
                dve.wait_ge(w_ps, n + 1)
                dve.wait_ge(g_sb, n + 1)
                for j in range(TPC):
                    k, cols = c * TPC + j, slice(j * D, (j + 1) * D)
                    op = dve.scalar_tensor_tensor(msg[:, cols], ps_w[:, cols], scale[:, k : k + 1], g[:, cols], ALU.mult, ALU.mult)
                op.then_inc(msg_sb, 1)

            def centre(n, c):
                for j in range(TPC):
                    k = c * TPC + j
                    op = dve.tensor_scalar(h[:, j * P : (j + 1) * P], rows_io[:, tile_cols(n * TPC + j)], mean[:, k : k + 1], 0.0, ALU.subtract, ALU.max)
                op.then_inc(h_done, 1)

            def lead(c, group):
                if c < STATS_STEPS:
                    for a in range(2 * c, min(2 * c + 2, GROUP)):
                        stats_of((group + 1) * GROUP + a, a, group + 1)
                else:
                    finish_stats(group + 1, c - STATS_STEPS)

            def step(n, c, group, first=False, final=False):
                dve.wait_ge(exp1, n + 1)
                dve.tensor_scalar(soft1[:, :], soft1[:, :], EXP_CAP, None, ALU.min).then_inc(cap1, 1)
                if not final:
                    lead(c, group)
                dve.wait_ge(log1, n + 1)
                dve.scalar_tensor_tensor(act1[:, :], ps_a1[:, :], b1_ln2[:, :], soft1[:, :], ALU.add, ALU.max).then_inc(act1_sb, 1)
                find_pairs(n, c, group, first)
                messages(n, c)
                if not (final and c == GROUP - 1):
                    if c == GROUP - 1:
                        finish_stats(group + 1, NEWTON)
                        enter_group(group + 1)
                    dve.wait_ge(hT_ps, n + 1)
                    centre(n + 1, (c + 1) % GROUP)
                if not first:
                    find_onward(n - 1, c)

            for c in range(GROUP):
                stats_of(c, c, 0)
            for part in range(NEWTON + 1):
                finish_stats(0, part)
            enter_group(0)
            centre(0, 0)
            for c in range(GROUP):
                step(c, c, 0, first=c == 0)
            with dve.Fori(1, GROUPS - 1) as group:
                for c in range(GROUP):
                    step(group * GROUP + c, c, group)
            for c in range(GROUP):
                step((GROUPS - 1) * GROUP + c, c, GROUPS - 1, final=True)
            dve.memset(again[:, :], 0.0).then_inc(onward_sb, 1)
            dve.wait_ge(onward_sb, CHUNKS)
            dve.wait_ge(picked_sb, CHUNKS)
            set_rows(CHUNKS - 1, last[:, 1, :])

            def half_block(b, u, group, parts=7, early=False):
                if parts & 1:
                    if not early:
                        dve.wait_ge(o_ps, b - 3)
                    dve.wait_ge(log2, b - 1)
                    k = u % 2
                    dve.scalar_tensor_tensor(act2[k][:, :], ps_z2[k][:, :], bo1_ln2[:, :], soft2[k][:, :], ALU.add, ALU.max).then_inc(act2_sb, 1)
                if parts & 2:
                    dve.wait_ge(exp2, b)
                    k = (u - 1) % 2
                    dve.tensor_scalar(soft2[k][:, :], soft2[k][:, :], EXP_CAP, None, ALU.min).then_inc(cap2, 1)
                if parts & 4:
                    v = (u - 3) % HGROUP
                    if v % 2 == 0:
                        dve.wait_ge(biased, (group if u >= 3 else group - 1) * BGROUP + v // 2 + 1)
                    dve.wait_ge(o_ps, b - 2)
                    rows = x_sb[:, v // 2, (v % 2) * CHUNK : (v % 2 + 1) * CHUNK]
                    dve.tensor_tensor(rows, ps_o[v % 2][:, :], rows, ALU.add).then_inc(added, 1)

            for u in range(1, HGROUP):
                half_block(u, u, 0, 2 if u < 2 else 3 if u < 3 else 7, early=u < 4)
            with dve.Fori(1, BGROUPS) as group:
                for u in range(HGROUP):
                    half_block(group * HGROUP + u, u, group)
            half_block(HALVES, 0, BGROUPS)
            half_block(HALVES + 1, 1, BGROUPS, 5)
            half_block(HALVES + 2, 2, BGROUPS, 4)


_INS = [
    "x", "src", "dst", "edge_attr_20", "edge_weight", "L0_gnn_W_in2f", "L0_gnn_W_f1", "L0_gnn_b_f1",
    "L0_gnn_W_f2", "L0_gnn_b_f2", "L0_gnn_W_o1", "L0_gnn_b_o1", "L0_gnn_W_o2", "L0_gnn_b_o2",
]


def kernel(**inputs):
    import numpy as _np
    import concourse.bacc as _bacc
    from concourse import mybir as _mybir
    from concourse.bass_utils import run_bass_kernel_spmd as _run

    nc = _bacc.Bacc("TRN2", target_bir_lowering=False, num_devices=1)
    arrays, args = {}, []
    for name in _INS:
        a = _np.ascontiguousarray(inputs[name])
        arrays[f"in_{name}_dram"] = a
        args.append(nc.dram_tensor(f"in_{name}_dram", a.shape, _mybir.dt.from_np(a.dtype), kind="ExternalInput").ap())
    args.append(nc.dram_tensor("out_0_dram", (NODES, D), F32, kind="ExternalOutput").ap())
    gnn_layer(nc, *args)
    r = _run(nc, [arrays], core_ids=[0])
    return r.results[0]["out_0_dram"]
```

```python
import math
from contextlib import ExitStack

import concourse.bass as bass
from concourse import mybir

F32 = mybir.dt.float32
BF16 = mybir.dt.bfloat16
I32 = mybir.dt.int32
ALU = mybir.AluOpType
ACT = mybir.ActivationFunctionType

P = 128
NODES = 100000
EDGES = 25000
D = 128
RBF = 20
LN_EPS = 1e-5
LN2 = math.log(2.0)
EXP_CAP = 2.0**60
RSQRT_MAGIC = float(0x5F3759DF)
NEWTON = 3

TPC = 4
CHUNK = TPC * P
CHUNKS = -(-EDGES // CHUNK)
TILES = CHUNKS * TPC
GROUP = 7
GROUPS = CHUNKS // GROUP
GT = GROUP * TPC
STATS_STEPS = 4
TAIL = EDGES - (CHUNKS - 1) * CHUNK

ZROWS = 2048
ZBLOCKS = -(-NODES // ZROWS)
DUMP = ZBLOCKS * ZROWS

PACED = 4
CLEARS = 2
assert PACED * GROUP < ZBLOCKS <= (PACED + 2 * CLEARS) * GROUP

ROWS = 1024
RPP = ROWS // P
BLOCK = RPP * D
BLOCKS = -(-NODES // ROWS)
HALVES = 2 * BLOCKS
SLOTS = 7
LAG = 2
BGROUP = SLOTS
BGROUPS = BLOCKS // BGROUP
HGROUP = 2 * BGROUP

assert STATS_STEPS < GROUP - 1 and 2 * STATS_STEPS >= GROUP
assert CHUNKS == GROUP * GROUPS and BLOCKS == BGROUP * BGROUPS and ROWS == 2 * TPC * P


def gnn_layer(nc, x, src, dst, edge_attr, edge_weight, w_in2f, w_f1, b_f1, w_f2, b_f2, w_o1, b_o1, w_o2, b_o2, out):
    agg = nc.dram_tensor("agg", (DUMP + CHUNK, D), F32, kind="Internal").ap()
    src_padded = nc.dram_tensor("src_padded", (CHUNKS, CHUNK), I32, kind="Internal").ap()

    with ExitStack() as ctx:

        def sb(name, shape, dt=F32):
            return ctx.enter_context(nc.sbuf_tensor(name, shape, dt))

        def ps(name):
            return ctx.enter_context(nc.psum_tensor(name, [P, CHUNK], F32))

        def sem(name):
            return ctx.enter_context(nc.semaphore(name))

        rows_io = sb("rows_io", [P, TILES * D])
        agg_in_sb = rows_io[:, 0 : SLOTS * BLOCK].rearrange("p (k f) -> p k f", k=SLOTS)
        x_sb = sb("x_sb", [P, SLOTS, BLOCK])
        feats = sb("feats", [P, CHUNKS, TPC * RBF])
        src_all = sb("src_all", [P, GROUP, CHUNK], I32)
        dst_idx = sb("dst_idx", [P, TILES], I32)
        agg_idx = sb("agg_idx", [P, TILES], I32)
        src_cols = sb("src_cols", [P, 2, TILES])
        weight = sb("weight", [P, TILES])
        dump_row = sb("dump_row", [P, TPC])
        dump_row_1 = sb("dump_row_1", [P, TPC])
        stats = sb("stats", [P, GT, 6])
        mean_2 = sb("mean_2", [P, GT])
        minus_mean = sb("minus_mean", [P, TILES])
        per_edge = sb("per_edge", [P, 3, GT])
        src_now, scale = per_edge[:, 0, :], per_edge[:, 2, :]
        count = sb("count", [P, TPC])
        again = sb("again", [P, TPC])
        last = sb("last", [P, 2, TPC])
        last_before = sb("last_before", [P, 2, TPC])
        last_bf = sb("last_bf", [P, TPC], BF16)
        picked = sb("picked", [P, TPC])
        var = sb("var", [P, GT])
        ln_a = sb("ln_a", [P, GT])
        ln_b = sb("ln_b", [P, GT])
        rsq = sb("rsq", [P, GT])
        h = sb("h", [P, CHUNK])
        hT = sb("hT", [P, CHUNK])
        g = sb("g", [P, CHUNK])
        feat_in = sb("feat_in", [P, TPC * RBF])
        featT = sb("featT", [TPC * RBF, P])
        soft1 = sb("soft1", [P, CHUNK])
        act1 = sb("act1", [P, CHUNK])
        msg = sb("msg", [P, CHUNK])
        pairs = [sb(f"pairs{j}", [P, CHUNK - j * P]) for j in range(TPC)]
        aggT = [sb(f"aggT{k}", [P, CHUNK]) for k in range(2)]
        soft2 = [sb(f"soft2{k}", [P, CHUNK]) for k in range(2)]
        act2 = [sb(f"act2{k}", [P, CHUNK]) for k in range(2)]
        onward = [None, aggT[0][:, 0:P], aggT[0][:, P : 3 * P], aggT[1][:, 0 : 3 * P]]
        ident = sb("ident", [P, P])
        ident_bf = sb("ident_bf", [P, P], BF16)
        ones_bf = sb("ones_bf", [P, P], BF16)
        w_in = sb("w_in", [P, D])
        w1_at = sb("w1_at", [TPC * RBF, TPC, D])
        w2 = sb("w2", [P, D])
        wo1 = sb("wo1", [P, D])
        wo2 = sb("wo2", [P, D])
        half = sb("half", [P, 1])
        b1 = sb("b1", [P, 1])
        bo1 = sb("bo1", [P, 1])
        b1_ln2 = sb("b1_ln2", [P, 1])
        bo1_ln2 = sb("bo1_ln2", [P, 1])
        b2_rows = sb("b2_rows", [P, D])
        bo2_rows = sb("bo2_rows", [P, D])
        b2_bf = [sb(f"b2_bf{i}", [P, D], BF16) for i in range(3)]
        b2_parts = sb("b2_parts", [P, TPC, D], BF16)

        dst_rows = hT[:, :].bitcast(I32)
        dst_rows_f = g
        src_rows = act1[:, :].bitcast(I32)
        src_rows_f = soft1
        weight_rows = msg
        zeros = x_sb[:, 0:2, :]
        pair_mask = x_sb[:, 2, 0:CHUNK]
        dump_i = x_sb[:, 3, 0:TPC].bitcast(I32)

        bank = [ps(f"bank{k}") for k in range(7)]
        ps_mask = ps("ps_mask")
        ps_hT, ps_g, ps_a1, ps_w, ps_sum, ps_last = bank[0:6]
        ps_fT = bank[6][0 : TPC * RBF, 0:P]
        ps_aggT, ps_z2, ps_o = bank[0:2], bank[2:4], bank[4:6]

        seen = sem("seen")
        s_mine = sem("s_mine")
        s_init = sem("s_init")
        s_dst = sem("s_dst")
        s_src = sem("s_src")
        s_pad = sem("s_pad")
        s_wts = sem("s_wts")
        s_par = sem("s_par")
        s_bias = sem("s_bias")
        s_feat = sem("s_feat")
        s_zero = sem("s_zero")
        s_ident = sem("s_ident")
        s_iota = sem("s_iota")
        s_prep = sem("s_prep")
        s_pprep = sem("s_pprep")
        agg_done = sem("agg_done")
        gathered = [sem(f"gathered{c}") for c in range(GROUP)]
        scattered = [sem(f"scattered{j}") for j in range(TPC)]
        src_in = [sem(f"src_in{c}") for c in range(GROUP)]
        x_in = [sem(f"x_in{k}") for k in range(SLOTS)]
        agg_in = [sem(f"agg_in{k}") for k in range(SLOTS)]
        stored = [sem(f"stored{k}") for k in range(SLOTS)]
        bn_done = sem("bn_done")
        ln_step = sem("ln_step")
        h_done = sem("h_done")
        hT_ps = sem("hT_ps")
        hT_sb = sem("hT_sb")
        g_ps = sem("g_ps")
        g_sb = sem("g_sb")
        feat_sb = sem("feat_sb")
        fT_ps = sem("fT_ps")
        fT_sb = sem("fT_sb")
        a1_ps = sem("a1_ps")
        exp1 = sem("exp1")
        cap1 = sem("cap1")
        log1 = sem("log1")
        act1_sb = sem("act1_sb")
        w_ps = sem("w_ps")
        pairs_sb = sem("pairs_sb")
        last_sb = sem("last_sb")
        last_ps = sem("last_ps")
        onward_sb = sem("onward_sb")
        picked_sb = sem("picked_sb")
        chosen = sem("chosen")
        rows_set = sem("rows_set")
        msg_sb = sem("msg_sb")
        paired = sem("paired")
        sum_ps = sem("sum_ps")
        msgs_ready = sem("msgs_ready")
        aggT_ps = sem("aggT_ps")
        aggT_sb = sem("aggT_sb")
        z2_ps = sem("z2_ps")
        exp2 = sem("exp2")
        cap2 = sem("cap2")
        log2 = sem("log2")
        act2_sb = sem("act2_sb")
        o_ps = sem("o_ps")
        added = sem("added")
        biased = sem("biased")

        block = ctx.enter_context(nc.Block())

        def tile_cols(t):
            return bass.ds(t * D, D)

        def block_rows(ap, m):
            at = min(m * ROWS, NODES - ROWS) if isinstance(m, int) else m * ROWS
            return ap[bass.ds(at, ROWS), :].rearrange("(p r) d -> p (r d)", p=P)

        full = CHUNKS - 1
        full_edges = full * CHUNK

        LN_STEPS = 6 + 3 * NEWTON

        @block.sync
        def _(sp):
            def load_rows(tile, v, s):
                sp.dma_start(tile[0:full, :], v[0:full_edges].rearrange("(n i) -> n i", i=CHUNK)).then_inc(s, 16)
                sp.dma_start(tile[full:CHUNKS, 0:TAIL], v[full_edges:EDGES].rearrange("(n i) -> n i", n=1)).then_inc(s, 16)

            sp.wait_ge(s_init, 1)
            load_rows(dst_rows, dst, s_dst)
            sp.wait_ge(s_init, 2)
            load_rows(src_rows, src, s_src)
            sp.wait_ge(s_init, 3)
            load_rows(weight_rows, edge_weight, s_wts)
            for tile, v in ((b1, b_f1), (bo1, b_o1)):
                sp.dma_start(tile[:, :], v.rearrange("(p a) -> p a", a=1)).then_inc(s_bias, 16)
            for tile, v in ((b2_rows, b_f2), (bo2_rows, b_o2)):
                sp.dma_start(tile[:, :], v.rearrange("(a d) -> a d", a=1).to_broadcast([P, D])).then_inc(s_bias, 16)
            for tile, v in ((w_in, w_in2f), (w2, w_f2), (wo1, w_o1), (wo2, w_o2)):
                sp.dma_start(tile[:, :], v[:, :]).then_inc(s_par, 16)
            sp.wait_ge(s_init, 5)
            for i in range(TPC):
                sp.dma_start(w1_at[i * RBF : (i + 1) * RBF, i, :], w_f1[:, :]).then_inc(s_par, 16)
            by_quad = edge_attr[0:full_edges, :].rearrange("(n q i) k -> q n (i k)", q=P, i=TPC)
            sp.dma_start(feats[:, 0:full, :], by_quad).then_inc(s_feat, 16)
            sp.dma_start(feats[0 : TAIL // TPC, full, :], edge_attr[full_edges:EDGES, :].rearrange("(q i) k -> q (i k)", i=TPC)).then_inc(s_feat, 16)
            sp.wait_ge(s_prep, 4)
            sp.dma_start(src_padded[:, :], src_rows[0:CHUNKS, :]).then_inc(s_pad, 16)
            sp.wait_ge(s_pad, 16)

            def load_src(n, c):
                sp.dma_start(src_all[:, c, :], src_padded[bass.ds(n, 1), :].to_broadcast([P, CHUNK])).then_inc(src_in[c], 16)

            for c in range(GROUP):
                load_src(c, c)
            sp.wait_ge(s_init, 6)

            def clear(zb):
                sp.dma_start(agg[bass.ds(zb * ZROWS, ZROWS), :].rearrange("(p r) d -> p (r d)", p=P), zeros).then_inc(s_zero, 16)

            dump = agg[DUMP : DUMP + CHUNK, :].rearrange("(p r) d -> p (r d)", p=P)
            sp.dma_start(dump, x_sb[:, 0, 0:CHUNK]).then_inc(s_zero, 16)

            def paced_clear(group, c):
                sp.wait_ge(gathered[c], (group + 1) * (16 * TPC))
                clear(group * GROUP + c)

            def next_src(n, c):
                sp.wait_ge(onward_sb, n - GROUP + 1)
                load_src(n, c)

            with sp.Fori(0, PACED - 1) as group:
                for c in range(GROUP):
                    paced_clear(group, c)
            for c in range(GROUP):
                next_src(GROUP + c, c)
                paced_clear(PACED - 1, c)
            for n in range(2 * GROUP, 4 * GROUP):
                next_src(n, n % GROUP)
                first = PACED * GROUP + (n - 2 * GROUP) * CLEARS
                for zb in range(first, min(first + CLEARS, ZBLOCKS)):
                    clear(zb)
            with sp.Fori(4, GROUPS) as group:
                for c in range(GROUP):
                    next_src(group * GROUP + c, c)

            def load_x(m, k):
                sp.dma_start(x_sb[:, k, :], block_rows(x, m)).then_inc(x_in[k], 16)

            def load_agg(m, k):
                sp.dma_start(agg_in_sb[:, k, :], block_rows(agg, m)).then_inc(agg_in[k], 16)

            sp.wait_ge(s_zero, 16 * (ZBLOCKS + 1))
            sp.wait_ge(s_prep, 6)
            for m in range(SLOTS):
                load_x(m, m)
            sp.wait_ge(agg_done, 1)
            for m in range(SLOTS):
                load_agg(m, m)

            def turn(group, first=False, last=False):
                for k in range(BGROUP):
                    m = group * BGROUP + k
                    sp.wait_ge(added, 2 * m + 2)
                    if last and k == BGROUP - 1:
                        sp.wait_ge(stored[k - 1], 16 * BGROUPS)
                    sp.dma_start(block_rows(out, m), x_sb[:, k, :]).then_inc(stored[k], 16)
                    back = k - LAG
                    if back >= 0:
                        sp.wait_ge(stored[back], group * 16 + 16)
                    elif not first:
                        sp.wait_ge(stored[back % BGROUP], group * 16)
                    if not (last and back >= 0) and not (first and back < 0):
                        load_x(m + SLOTS - LAG, back % BGROUP)
                        load_agg(m + SLOTS - LAG, back % BGROUP)

            turn(0, first=True)
            with sp.Fori(1, BGROUPS - 1) as group:
                turn(group)
            turn(BGROUPS - 1, last=True)
            for k in range(BGROUP - LAG, BGROUP):
                sp.wait_ge(stored[k], 16 * BGROUPS)

        @block.gpsimd
        def _(gp):
            gp.memset(ident[:, :], 0.0).then_inc(s_ident, 1)
            gp.memset(pair_mask, 0.0).then_inc(s_ident, 1)
            gp.memset(ident_bf[:, :], 0.0).then_inc(s_ident, 1)
            gp.wait_ge(s_ident, 3)
            gp.affine_select(out=ident_bf[:, :], in_=ident_bf[:, :], compare_op=ALU.not_equal, fill=1.0, base=0, pattern=[[-1, P]], channel_multiplier=1).then_inc(s_ident, 1)
            gp.affine_select(out=ident[:, :], in_=ident[:, :], compare_op=ALU.not_equal, fill=1.0, base=0, pattern=[[-1, P]], channel_multiplier=1).then_inc(s_ident, 1)
            gp.affine_select(out=pair_mask, in_=pair_mask, compare_op=ALU.is_ge, fill=1.0, base=-1, pattern=[[-1, CHUNK]], channel_multiplier=1).then_inc(s_ident, 1)
            gp.iota(dump_i, pattern=[[P, TPC]], base=DUMP, channel_multiplier=1).then_inc(s_iota, 1)
            gp.memset(ones_bf[:, :], 1.0).then_inc(s_iota, 1)

            gp.wait_ge(s_prep, 2)
            for t in range(TILES):
                chunk = t // TPC
                c = chunk % GROUP
                if t % TPC == 0 and chunk >= GROUP:
                    gp.wait_ge(gathered[c], 16 * TPC * (chunk // GROUP))
                gp.indirect_dma_start(
                    rows_io[:, t * D : (t + 1) * D], None, x[:, :], bass.IndirectOffsetOnAxis(dst_idx[:, t : t + 1], 0)
                ).then_inc(gathered[c], 16)

            gp.wait_ge(s_zero, 16 * (ZBLOCKS + 1))
            for t in range(TILES):
                chunk, j = divmod(t, TPC)
                if j == 0:
                    gp.wait_ge(msgs_ready, chunk + 1)
                    gp.wait_ge(rows_set, chunk + 1)
                if chunk:
                    gp.wait_ge(scattered[j], 16 * chunk)
                gp.indirect_dma_start(
                    agg[:, :], bass.IndirectOffsetOnAxis(agg_idx[:, t : t + 1], 0), rows_io[:, t * D : (t + 1) * D], None, compute_op=ALU.add
                ).then_inc(scattered[j], 16)
            for j in range(TPC):
                gp.wait_ge(scattered[j], 16 * CHUNKS)
            gp.sem_inc(agg_done, 1)

            with gp.Fori(0, BGROUPS) as group:
                for k in range(BGROUP):
                    gp.wait_ge(x_in[k], group * 16 + 16)
                    rows = x_sb[:, k, :].rearrange("p (r d) -> p r d", d=D)
                    gp.tensor_tensor(rows, rows, bo2_rows[:, :].rearrange("p (a d) -> p a d", a=1).to_broadcast([P, RPP, D]), ALU.add).then_inc(biased, 1)

        @block.scalar
        def _(act):
            def copy_feats(n):
                act.activation(feat_in[:, :], feats[:, bass.ds(n, 1), :].rearrange("q n k -> q (n k)"), ACT.Copy).then_inc(feat_sb, 1)

            def evac_featT(n):
                act.wait_ge(fT_ps, n + 1)
                act.activation(featT[:, :], ps_fT, ACT.Copy).then_inc(fT_sb, 1)

            def exp_1(n):
                act.wait_ge(a1_ps, n + 1)
                act.activation(soft1[:, :], ps_a1[:, :], ACT.Exp, bias=b1[:, :]).then_inc(exp1, 1)

            def log_1(n):
                act.wait_ge(cap1, n + 1)
                act.activation(soft1[:, :], soft1[:, :], ACT.Ln, bias=half[:, :], scale=0.5).then_inc(log1, 1)

            def evac_hT(n):
                act.wait_ge(hT_ps, n + 1)
                act.activation(hT[:, :], ps_hT[:, :], ACT.Copy).then_inc(hT_sb, 1)

            def evac_g(n, first=False):
                if not first:
                    act.wait_ge(msg_sb, TPC * n)
                act.wait_ge(g_ps, n + 1)
                act.activation(g[:, :], ps_g[:, :], ACT.Copy).then_inc(g_sb, 1)

            def evac_sum(n):
                act.wait_ge(sum_ps, n + 1)
                act.sem_inc(seen, 1)
                act.activation(rows_io[:, bass.ds(n * CHUNK, CHUNK)], ps_sum[:, :], ACT.Copy).then_inc(msgs_ready, 1)

            def centre(n):
                for j in range(TPC):
                    t = n * TPC + j
                    op = act.activation(h[:, j * P : (j + 1) * P], rows_io[:, tile_cols(t)], ACT.Relu, bias=minus_mean[:, bass.ds(t, 1)])
                op.then_inc(h_done, 1)

            def step(n, first=False, ahead=2):
                log_1(n)
                evac_hT(n)
                if ahead >= 1:
                    evac_featT(n + 1)
                if ahead >= 2:
                    copy_feats(n + 2)
                if not first:
                    evac_sum(n - 1)
                evac_g(n, first)
                if ahead >= 1:
                    exp_1(n + 1)
                    centre(n + 1)

            act.preload_act_table_set("natural_log_exp_and_others")
            act.wait_ge(s_feat, 32)
            act.wait_ge(s_init, 7)
            act.wait_ge(s_bias, 64)
            copy_feats(0)
            evac_featT(0)
            copy_feats(1)
            exp_1(0)
            act.wait_ge(ln_step, LN_STEPS)
            centre(0)
            step(0, first=True)
            with act.Fori(1, CHUNKS - 2) as n:
                step(n)
            step(CHUNKS - 2, ahead=1)
            step(CHUNKS - 1, ahead=0)
            evac_sum(CHUNKS - 1)

            def half_block(b, u, parts=3):
                k = u % 2
                if parts & 2:
                    act.wait_ge(z2_ps, b - 1)
                    act.activation(soft2[k][:, :], ps_z2[k][:, :], ACT.Exp, bias=bo1[:, :]).then_inc(exp2, 1)
                if parts & 1:
                    act.wait_ge(aggT_ps, b + 1)
                    act.activation(aggT[k][:, :], ps_aggT[k][:, :], ACT.Copy).then_inc(aggT_sb, 1)
                if parts & 2:
                    act.wait_ge(cap2, b - 1)
                    act.activation(soft2[k][:, :], soft2[k][:, :], ACT.Ln, bias=half[:, :], scale=0.5).then_inc(log2, 1)

            for u in range(HGROUP):
                half_block(u, u, 1 if u < 2 else 3)
            with act.Fori(1, BGROUPS) as group:
                for u in range(HGROUP):
                    half_block(group * HGROUP + u, u)
            half_block(HALVES, 0, 2)
            half_block(HALVES + 1, 1, 2)

        @block.tensor
        def _(pe):
            def transpose_feats(n):
                pe.wait_ge(feat_sb, n + 1)
                pe.transpose(ps_fT, feat_in[:, :], ident[:, :]).then_inc(fT_ps, 1)

            def filter_1(n, first=False):
                if not first:
                    pe.wait_ge(act1_sb, n)
                pe.wait_ge(fT_sb, n + 1)
                for i in range(TPC):
                    mm = pe.matmul(ps_a1[:, i::TPC], w1_at[:, i, :], featT[:, :], start=True, stop=True)
                mm.then_inc(a1_ps, 1)

            def rows_product(bank, lhs, w, parts=None):
                if parts is not None:
                    pe.matmul(bank[:, :], ones_bf[:, :], parts, start=True, stop=True)
                for j in range(TPC):
                    tile = bank[:, j * D : (j + 1) * D]
                    mm = pe.matmul(tile, lhs[:, j * P : (j + 1) * P], w[:, :], start=parts is None, stop=True, skip_group_check=parts is not None)
                return mm

            def filter_2(n, first=False):
                if not first:
                    pe.wait_ge(msg_sb, TPC * n)
                pe.wait_ge(act1_sb, n + 1)
                rows_product(ps_w, act1, w2, b2_parts[:, :, :].rearrange("p j d -> p (j d)")).then_inc(w_ps, 1)

            def transpose_h(n):
                pe.wait_ge(h_done, n + 1)
                for j in range(TPC):
                    tr = pe.transpose(ps_hT[:, j * P : (j + 1) * P], h[:, j * P : (j + 1) * P], ident[:, :])
                tr.then_inc(hT_ps, 1)

            def in2f(n, first=False):
                if not first:
                    pe.wait_ge(g_sb, n)
                pe.wait_ge(hT_sb, n + 1)
                rows_product(ps_g, hT, w_in).then_inc(g_ps, 1)

            def sum_pairs(n, first=False):
                if not first:
                    pe.wait_ge(msgs_ready, n)
                pe.wait_ge(pairs_sb, n + 1)
                for to in range(TPC):
                    pe.wait_ge(msg_sb, TPC * n + to + 1)
                    for j in range(to + 1):
                        at = (to - j) * P
                        mm = pe.matmul(
                            ps_sum[:, to * D : (to + 1) * D], pairs[j][:, at : at + P], msg[:, j * D : (j + 1) * D],
                            start=to == 0, stop=True, skip_group_check=True,
                        )
                mm.then_inc(paired, 1)
                if first:
                    pe.nop().then_inc(sum_ps, 1)

            def sum_onward(n):
                pe.wait_ge(onward_sb, n)
                for to in range(TPC - 1):
                    for i in range(to + 1, TPC):
                        sent = rows_io[:, bass.ds((n - 1) * CHUNK + i * D, D)]
                        mm = pe.matmul(ps_sum[:, to * D : (to + 1) * D], onward[i][:, to * P : (to + 1) * P], sent, start=False, stop=True, skip_group_check=True)
                mm.then_inc(sum_ps, 1)

            def spread_last(n):
                pe.wait_ge(last_sb, n + 1)
                for j in range(TPC - 1):
                    mm = pe.matmul(ps_last[:, j * P : (j + 1) * P], last_bf[:, j : j + 1].to_broadcast([P, P]), ident_bf[:, :], start=True, stop=True)
                mm.then_inc(last_ps, 1)

            def step(n, first=False, second=False, ahead=True):
                if not first:
                    sum_pairs(n - 1, first=second)
                transpose_h(n)
                if ahead:
                    transpose_feats(n + 1)
                if not first and not second:
                    sum_onward(n - 1)
                in2f(n, first)
                filter_2(n, first)
                if not first:
                    spread_last(n)
                if ahead:
                    filter_1(n + 1)

            pe.wait_ge(s_ident, 6)
            for k, rows in enumerate((dst_rows_f, src_rows_f, weight_rows)):
                if k < 2:
                    pe.wait_ge(s_prep, (1, 3)[k])
                else:
                    pe.wait_ge(s_wts, 32)
                for j in range(TPC):
                    tr = pe.transpose(bank[k][:, j * CHUNKS : (j + 1) * CHUNKS], rows[0:CHUNKS, j * P : (j + 1) * P], ident[0:CHUNKS, 0:CHUNKS])
                tr.then_inc(s_pprep, 1)
            pe.wait_ge(s_par, 16 * 8)
            pe.wait_ge(s_prep, 6)
            pe.wait_ge(s_iota, 2)
            transpose_feats(0)
            filter_1(0, first=True)
            step(0, first=True)
            step(1, second=True)
            with pe.Fori(2, CHUNKS - 1) as n:
                step(n)
            step(CHUNKS - 1, ahead=False)
            sum_pairs(CHUNKS - 1)
            sum_onward(CHUNKS - 1)

            def half_block(b, u, group, parts=7, early=False, first=False):
                k = u % 2
                if parts & 2:
                    if not first:
                        pe.wait_ge(act2_sb, b - 3)
                    pe.wait_ge(aggT_sb, b - 1)
                    pe.matmul(ps_z2[k][:, :], wo1[:, :], aggT[k][:, :], start=True, stop=True).then_inc(z2_ps, 1)
                if parts & 1:
                    slot = u // 2
                    if k == 0:
                        pe.wait_ge(agg_in[slot], group * 16 + 16)
                    for j in range(TPC):
                        at = (k * TPC + j) * D
                        tr = pe.transpose(ps_aggT[k][:, j * P : (j + 1) * P], agg_in_sb[:, slot, at : at + D], ident[:, :])
                    tr.then_inc(aggT_ps, 1)
                if parts & 4:
                    if not early:
                        pe.wait_ge(added, b - 5)
                    pe.wait_ge(act2_sb, b - 3)
                    rows_product(ps_o[k], act2[k], wo2).then_inc(o_ps, 1)

            pe.wait_ge(msgs_ready, CHUNKS)
            for u in range(HGROUP):
                half_block(u, u, 0, 1 if u < 2 else 3 if u < 4 else 7, early=u < 6, first=u < 4)
            with pe.Fori(1, BGROUPS) as group:
                for u in range(HGROUP):
                    half_block(group * HGROUP + u, u, group)
            half_block(HALVES, 0, None, 6)
            half_block(HALVES + 1, 1, None, 6)
            half_block(HALVES + 2, 2, None, 4)
            half_block(HALVES + 3, 3, None, 4)

        @block.vector
        def _(dve):
            dve.memset(dst_rows, 0).then_inc(s_init, 1)
            dve.memset(src_rows, DUMP + CHUNK - 1).then_inc(s_init, 1)
            dve.memset(weight_rows[:, :], 0.0).then_inc(s_init, 1)
            dve.memset(w1_at[:, :, :], 0.0).then_inc(s_init, 1)
            dve.memset(feats[:, full, :], 0.0).then_inc(s_init, 1)
            dve.memset(zeros, 0.0).then_inc(s_init, 1)
            dve.memset(half[:, :], 0.5).then_inc(s_init, 1)
            mine = 0

            def own(instruction):
                nonlocal mine
                mine += 1
                instruction.then_inc(s_mine, 1)
                dve.wait_ge(s_mine, mine)

            def columns(table, bank):
                return dve.tensor_copy(table.rearrange("p (n j) -> p n j", j=TPC), bank[:, 0:TILES].rearrange("p (j n) -> p n j", j=TPC))

            dve.wait_ge(s_dst, 32)
            dve.tensor_copy(dst_rows_f[0:CHUNKS, :], dst_rows[0:CHUNKS, :]).then_inc(s_prep, 1)
            dve.wait_ge(s_pprep, 1)
            columns(dst_idx[:, :], bank[0]).then_inc(s_prep, 1)
            dve.wait_ge(s_src, 32)
            dve.tensor_scalar(src_rows_f[0:CHUNKS, :], src_rows[0:CHUNKS, :], 1.0, None, ALU.add).then_inc(s_prep, 1)
            dve.wait_ge(s_prep, 3)
            dve.tensor_copy(src_rows[0:CHUNKS, :], src_rows_f[0:CHUNKS, :]).then_inc(s_prep, 1)
            dve.wait_ge(s_ident, 6)
            own(dve.tensor_copy(ps_mask[:, :], pair_mask))
            dve.wait_ge(s_iota, 1)
            own(dve.tensor_copy(dump_row[:, :], dump_i))
            own(dve.tensor_scalar(dump_row_1[:, :], dump_row[:, :], 1.0, None, ALU.add))
            dve.wait_ge(s_pprep, 3)
            own(columns(src_cols[:, 0, :], bank[1]))
            tiles = "p (n j) -> p n j"
            own(dve.tensor_tensor(
                src_cols[:, 1, :].rearrange(tiles, j=TPC), src_cols[:, 0, :].rearrange(tiles, j=TPC),
                dump_row_1[:, :].rearrange("p (a j) -> p a j", a=1).to_broadcast([P, CHUNKS, TPC]), ALU.subtract,
            ))
            columns(weight[:, :], bank[2]).then_inc(s_prep, 1)
            dve.wait_ge(s_bias, 64)
            own(dve.tensor_scalar(b1_ln2[:, :], b1[:, :], -LN2, None, ALU.add))
            own(dve.tensor_scalar(bo1_ln2[:, :], bo1[:, :], -LN2, None, ALU.add))
            own(dve.memset(b2_parts[:, :, :], 0.0))
            for i in range(3):
                own(dve.tensor_copy(b2_bf[i][:, :], b2_rows[:, :]))
                if i < 2:
                    own(dve.tensor_tensor(b2_rows[:, :], b2_rows[:, :], b2_bf[i][:, :], ALU.subtract))
                one = slice(32 * i, 32 * i + 1)
                own(dve.tensor_copy(b2_parts[one, :, :], b2_bf[i][one, :].rearrange("p (a d) -> p a d", a=1).to_broadcast([1, TPC, D])))
            own(dve.memset(again[:, :], 0.0))
            dve.wait_ge(s_pad, 16)
            dve.wait_ge(s_prep, 5)
            dve.nop().then_inc(s_prep, 1)

            def stats_of(n, c, group):
                dve.wait_ge(gathered[c], 16 * TPC * (group + 1))
                for j in range(TPC):
                    bn = dve.bn_stats(stats[:, c * TPC + j, :], rows_io[:, tile_cols(n * TPC + j)])
                bn.then_inc(bn_done, 1)

            def finish_stats(group, part):
                k = 0

                def settle(instruction):
                    nonlocal k
                    k += 1
                    instruction.then_inc(ln_step, 1)
                    dve.wait_ge(ln_step, group * LN_STEPS + k)

                def newton():
                    settle(dve.tensor_tensor(ln_a[:, :], rsq[:, :], rsq[:, :], ALU.mult))
                    settle(dve.scalar_tensor_tensor(ln_a[:, :], ln_a[:, :], -0.5, var[:, :], ALU.mult, ALU.mult))
                    settle(dve.scalar_tensor_tensor(rsq[:, :], ln_a[:, :], 1.5, rsq[:, :], ALU.add, ALU.mult))

                if part == 0:
                    mean0, mean1, m20, m21 = (stats[:, :, i] for i in (1, 4, 2, 5))
                    dve.wait_ge(bn_done, (group + 1) * GROUP)
                    dve.tensor_tensor(var[:, :], m20, m21, ALU.add)
                    dve.tensor_tensor(mean_2[:, :], mean0, mean1, ALU.add)
                    settle(dve.tensor_tensor(ln_a[:, :], mean0, mean1, ALU.subtract))
                    dve.tensor_scalar(minus_mean[:, bass.ds(group * GT, GT)], mean_2[:, :], -0.5, None, ALU.mult)
                    dve.tensor_scalar(var[:, :], var[:, :], 1.0 / D, LN_EPS, ALU.mult, ALU.add)
                    settle(dve.scalar_tensor_tensor(ln_a[:, :], ln_a[:, :], 0.25, ln_a[:, :], ALU.mult, ALU.mult))
                    settle(dve.tensor_tensor(var[:, :], var[:, :], ln_a[:, :], ALU.add))
                    settle(dve.tensor_single_scalar(ln_b[:, :].bitcast(I32), var[:, :].bitcast(I32), 1, ALU.logical_shift_right))
                    settle(dve.tensor_scalar(rsq[:, :].bitcast(I32), ln_b[:, :].bitcast(I32), -1.0, RSQRT_MAGIC, ALU.mult, ALU.add))
                else:
                    k = 5 + 3 * (part - 1)
                    newton()

            def enter_group(group):
                tiles_of = bass.ds(group * GT, GT)
                dve.tensor_copy(per_edge[:, 0:2, :], src_cols[:, :, tiles_of])
                dve.tensor_tensor(scale, rsq[:, :], weight[:, tiles_of], ALU.mult).then_inc(ln_step, 1)
                dve.wait_ge(ln_step, (group + 1) * LN_STEPS)

            def find_pairs(n, c, group, first=False):
                dve.wait_ge(src_in[c], group * 16 + 16)
                if not first:
                    dve.tensor_copy(last_before[:, :, :], last[:, :, :])
                    dve.wait_ge(paired, n)
                for j in range(TPC):
                    k = c * TPC + j
                    op = dve.scalar_tensor_tensor(
                        pairs[j][:, :], src_all[:, c, j * P :], src_now[:, k : k + 1], ps_mask[:, 0 : CHUNK - j * P],
                        ALU.is_equal, ALU.mult, accum_out=count[:, j : j + 1],
                    )
                op.then_inc(pairs_sb, 1)
                dve.wait_ge(pairs_sb, n + 1)
                now = slice(c * TPC, (c + 1) * TPC)
                twice = count[:, :].rearrange("p (a j) -> p a j", a=1).to_broadcast([P, 2, TPC])
                dve.tensor_scalar(last_bf[:, :], count[:, :], 1.0, None, ALU.is_equal).then_inc(last_sb, 1)
                dve.scalar_tensor_tensor(last[:, :, :], twice, 1.0, per_edge[:, 0:2, now], ALU.is_equal, ALU.mult).then_inc(picked_sb, 1)

            def find_onward(n, c):
                dve.wait_ge(last_ps, n + 1)
                dve.wait_ge(picked_sb, n + 2)
                dve.wait_ge(sum_ps, n + 1)
                for i in range(1, TPC):
                    op = dve.scalar_tensor_tensor(
                        onward[i], src_all[:, c, 0 : i * P], last_before[:, 0, i : i + 1], ps_last[:, 0 : i * P],
                        ALU.is_equal, ALU.mult, accum_out=again[:, i : i + 1],
                    )
                op.then_inc(onward_sb, 1)
                dve.wait_ge(onward_sb, n + 1)
                set_rows(n, last_before[:, 1, :])

            def set_rows(n, of_last):
                dve.scalar_tensor_tensor(picked[:, :], again[:, :], 0.0, of_last, ALU.is_equal, ALU.mult).then_inc(chosen, 1)
                dve.wait_ge(chosen, n + 1)
                dve.tensor_tensor(agg_idx[:, bass.ds(n * TPC, TPC)], picked[:, :], dump_row[:, :], ALU.add).then_inc(rows_set, 1)

            def messages(n, c):
                dve.wait_ge(w_ps, n + 1)
                dve.wait_ge(g_sb, n + 1)
                for j in range(TPC):
                    k, cols = c * TPC + j, slice(j * D, (j + 1) * D)
                    dve.scalar_tensor_tensor(msg[:, cols], ps_w[:, cols], scale[:, k : k + 1], g[:, cols], ALU.mult, ALU.mult).then_inc(msg_sb, 1)

            def lead(c, group):
                if c < STATS_STEPS:
                    for a in range(2 * c, min(2 * c + 2, GROUP)):
                        stats_of((group + 1) * GROUP + a, a, group + 1)
                elif c == STATS_STEPS:
                    finish_stats(group + 1, 0)
                else:
                    left, at = GROUP - 1 - STATS_STEPS, c - STATS_STEPS - 1
                    for part in range(-(-NEWTON * at // left), -(-NEWTON * (at + 1) // left)):
                        finish_stats(group + 1, 1 + part)

            def step(n, c, group, first=False, final=False):
                dve.wait_ge(exp1, n + 1)
                dve.tensor_scalar(soft1[:, :], soft1[:, :], EXP_CAP, None, ALU.min).then_inc(cap1, 1)
                if not final:
                    lead(c, group)
                dve.wait_ge(log1, n + 1)
                dve.scalar_tensor_tensor(act1[:, :], ps_a1[:, :], b1_ln2[:, :], soft1[:, :], ALU.add, ALU.max).then_inc(act1_sb, 1)
                find_pairs(n, c, group, first)
                messages(n, c)
                if not first:
                    find_onward(n - 1, c)
                if not final and c == GROUP - 1:
                    dve.wait_ge(msg_sb, TPC * (n + 1))
                    enter_group(group + 1)

            for c in range(GROUP):
                stats_of(c, c, 0)
            for part in range(NEWTON + 1):
                finish_stats(0, part)
            enter_group(0)
            for c in range(GROUP):
                step(c, c, 0, first=c == 0)
            with dve.Fori(1, GROUPS - 1) as group:
                for c in range(GROUP):
                    step(group * GROUP + c, c, group)
            for c in range(GROUP):
                step((GROUPS - 1) * GROUP + c, c, GROUPS - 1, final=True)
            dve.memset(again[:, :], 0.0).then_inc(onward_sb, 1)
            dve.wait_ge(onward_sb, CHUNKS)
            dve.wait_ge(picked_sb, CHUNKS)
            set_rows(CHUNKS - 1, last[:, 1, :])

            def half_block(b, u, group, parts=3):
                k = u % 2
                if parts & 1:
                    dve.wait_ge(exp2, b - 1)
                    dve.tensor_scalar(soft2[k][:, :], soft2[k][:, :], EXP_CAP, None, ALU.min).then_inc(cap2, 1)
                if parts & 2:
                    slot = (u // 2 - 2) % BGROUP
                    if k == 0:
                        dve.wait_ge(biased, (group if u >= 4 else group - 1) * BGROUP + slot + 1)
                    dve.wait_ge(o_ps, b - 3)
                    rows = x_sb[:, slot, k * CHUNK : (k + 1) * CHUNK]
                    dve.tensor_tensor(rows, ps_o[k][:, :], rows, ALU.add).then_inc(added, 1)
                if parts & 1:
                    dve.wait_ge(log2, b - 1)
                    dve.scalar_tensor_tensor(act2[k][:, :], ps_z2[k][:, :], bo1_ln2[:, :], soft2[k][:, :], ALU.add, ALU.max).then_inc(act2_sb, 1)

            for u in range(2, HGROUP):
                half_block(u, u, 0, 1 if u < 4 else 3)
            with dve.Fori(1, BGROUPS) as group:
                for u in range(HGROUP):
                    half_block(group * HGROUP + u, u, group)
            half_block(HALVES, 0, BGROUPS)
            half_block(HALVES + 1, 1, BGROUPS)
            half_block(HALVES + 2, 2, BGROUPS, 2)
            half_block(HALVES + 3, 3, BGROUPS, 2)


_INS = [
    "x", "src", "dst", "edge_attr_20", "edge_weight", "L0_gnn_W_in2f", "L0_gnn_W_f1", "L0_gnn_b_f1",
    "L0_gnn_W_f2", "L0_gnn_b_f2", "L0_gnn_W_o1", "L0_gnn_b_o1", "L0_gnn_W_o2", "L0_gnn_b_o2",
]


def kernel(**inputs):
    import numpy as _np
    import concourse.bacc as _bacc
    from concourse import mybir as _mybir
    from concourse.bass_utils import run_bass_kernel_spmd as _run

    nc = _bacc.Bacc("TRN2", target_bir_lowering=False, num_devices=1)
    arrays, args = {}, []
    for name in _INS:
        a = _np.ascontiguousarray(inputs[name])
        arrays[f"in_{name}_dram"] = a
        args.append(nc.dram_tensor(f"in_{name}_dram", a.shape, _mybir.dt.from_np(a.dtype), kind="ExternalInput").ap())
    args.append(nc.dram_tensor("out_0_dram", (NODES, D), F32, kind="ExternalOutput").ap())
    gnn_layer(nc, *args)
    r = _run(nc, [arrays], core_ids=[0])
    return r.results[0]["out_0_dram"]
```
